# Optimizing a Trainium2 kernel written in Bass

```python
import numpy as np
import jax
import jax.numpy as jnp

def _softmax(x, axis=-1):
    return jax.nn.softmax(x, axis=axis)

def _gelu(x):
    return jax.nn.gelu(x, approximate=True)

def _silu(x):
    return jax.nn.silu(x)

def _sigmoid(x):
    return jax.nn.sigmoid(x)

def _layernorm(x, axis=-1, eps=1e-05):
    m = jnp.mean(x, axis=axis, keepdims=True)
    v = jnp.var(x, axis=axis, keepdims=True)
    return (x - m) / jnp.sqrt(v + eps)

def _scatter_add(tgt, idx, src, axis=0):
    return tgt.at[idx].add(src)

def _segment_sum(src, seg, n):
    return jax.ops.segment_sum(src, seg, n)
kernel_name = 'mk_cond_seq_d2_seqx_r4_04f29e'

def setup_inputs(seed: int=0):
    np.random.seed(seed)
    _w = jnp.asarray

    def _rec_inputs():
        import jax
        import jax.numpy as jnp
        _rk = jax.random.key(seed)
        x = -0.0002928 + 1 * jax.random.normal(jax.random.fold_in(_rk, 1), (8, 512, 256), jnp.float32)
        _lenS = 512 - jax.random.randint(jax.random.fold_in(_rk, 7), (8,), 0, max(1, 512 // 4) + 1, jnp.int32)
        _lenS2 = 512 - jax.random.randint(jax.random.fold_in(_rk, 8), (8,), 0, max(1, 512 // 4) + 1, jnp.int32)
        itok_B_0_7 = jax.random.randint(jax.random.fold_in(_rk, 11), (8,), 0, 8, jnp.int32)
        itok_B_34_63 = jax.random.randint(jax.random.fold_in(_rk, 13), (8,), 34, 64, jnp.int32)
        fside_Bx16xSxS_0 = -1.47943e-05 + 1.00017 * jax.random.normal(jax.random.fold_in(_rk, 14), (8, 16, 512, 512), jnp.float32)
        _validS = jnp.arange(512)[None, :] < _lenS[:, None]
        _validS2 = jnp.arange(512)[None, :] < _lenS2[:, None]
        _causal = jnp.tril(jnp.ones((512, 512), dtype=bool))
        mask_Bx1xSxS_bk0 = jnp.logical_not(jnp.broadcast_to(_validS[:, None, None, :], (8, 1, 512, 512)))
        return (x, itok_B_0_7, itok_B_34_63, fside_Bx16xSxS_0, mask_Bx1xSxS_bk0)
    x, itok_B_0_7, itok_B_34_63, fside_Bx16xSxS_0, mask_Bx1xSxS_bk0 = _rec_inputs()

    def _L0_cond_setup():
        import jax, jax.numpy as jnp
        import numpy as np
        E, H, I = (8, 256, 1024)
        B, S = (4, 256)
        LN_EPS = 1e-12
        key = jax.random.key(seed)
        ks = jax.random.split(key, 8)
        x = jax.random.normal(ks[0], (B, S, H), dtype=jnp.float32)
        expert_idx = jax.random.randint(ks[1], (B,), 0, E, dtype=jnp.int64)
        Wi = jax.random.normal(ks[2], (E, H, I), dtype=jnp.float32) * 0.02
        bi = jnp.zeros((E, I), dtype=jnp.float32)
        Wo = jax.random.normal(ks[3], (E, I, H), dtype=jnp.float32) * 0.02
        bo = jnp.zeros((E, H), dtype=jnp.float32)
        gamma = jnp.ones((E, H), dtype=jnp.float32)
        beta = jnp.zeros((E, H), dtype=jnp.float32)
        return {'input_tensor': x, 'expert_idx': expert_idx, 'Wi': Wi, 'bi': bi, 'Wo': Wo, 'bo': bo, 'gamma': gamma, 'beta': beta}
    _L0_cond_all = _L0_cond_setup()
    _L0_cond_in = {k: v for k, v in _L0_cond_all.items() if k in ('Wi', 'bi', 'Wo', 'bo', 'gamma', 'beta')}
    del _L0_cond_all

    def _L1_cond_setup():
        import jax, jax.numpy as jnp
        import numpy as np
        import math
        D_MODEL = 256
        N_HEAD = 16
        HEAD_DIM = D_MODEL // N_HEAD
        D_FF = 1024
        NUM_STEPS = 100.0
        RESCALE = 4000.0
        EPS = 1e-05

        def _sin_emb(t):
            half = D_MODEL // 2
            x = t.astype(jnp.float32) / NUM_STEPS * RESCALE
            freqs = jnp.exp(jnp.arange(half, dtype=jnp.float32) * (-math.log(10000.0) / (half - 1)))
            e = x[:, None] * freqs[None, :]
            return jnp.concatenate([jnp.sin(e), jnp.cos(e)], axis=-1)

        def _ln(x):
            m = jnp.mean(x, axis=-1, keepdims=True)
            v = jnp.var(x, axis=-1, keepdims=True)
            return (x - m) / jnp.sqrt(v + EPS)

        def _gelu2(x):
            return x * jax.nn.sigmoid(1.702 * x)
        key = jax.random.key(seed)
        ks = jax.random.split(key, 24)
        B, S, D, F = (4, 128, D_MODEL, D_FF)
        std = 0.02
        inp = {'src': jax.random.normal(ks[0], (B, S, D), dtype=jnp.float32), 'src_mask': jax.random.randint(ks[1], (B, 1, S, S), 0, 2).astype(bool), 'timestep': jax.random.randint(ks[2], (B,), 0, 100, dtype=jnp.int32), 'attention_bias': jax.random.normal(ks[3], (B, N_HEAD, S, S), dtype=jnp.float32), 'W_ada': jax.random.normal(ks[4], (D, 2 * D), dtype=jnp.float32) * std, 'b_ada': jnp.zeros((2 * D,), dtype=jnp.float32), 'Wq': jax.random.normal(ks[5], (D, D), dtype=jnp.float32) * std, 'bq': jnp.zeros((D,), dtype=jnp.float32), 'Wk': jax.random.normal(ks[6], (D, D), dtype=jnp.float32) * std, 'bk': jnp.zeros((D,), dtype=jnp.float32), 'Wv': jax.random.normal(ks[7], (D, D), dtype=jnp.float32) * std, 'bv': jnp.zeros((D,), dtype=jnp.float32), 'Wo': jax.random.normal(ks[8], (D, D), dtype=jnp.float32) * std, 'bo': jnp.zeros((D,), dtype=jnp.float32), 'W1': jax.random.normal(ks[9], (D, F), dtype=jnp.float32) * std, 'b1': jnp.zeros((F,), dtype=jnp.float32), 'W2': jax.random.normal(ks[10], (F, D), dtype=jnp.float32) * std, 'b2': jnp.zeros((D,), dtype=jnp.float32), 'g2': jnp.ones((D,), dtype=jnp.float32), 'beta2': jnp.zeros((D,), dtype=jnp.float32)}
        return inp
    _L1_cond_all = _L1_cond_setup()
    _L1_cond_in = {k: v for k, v in _L1_cond_all.items() if k in ('W_ada', 'b_ada', 'Wq', 'bq', 'Wk', 'bk', 'Wv', 'bv', 'Wo', 'bo', 'W1', 'b1', 'W2', 'b2', 'g2', 'beta2')}
    del _L1_cond_all
    return {'x': x, 'itok_B_0_7': itok_B_0_7, 'itok_B_34_63': itok_B_34_63, 'fside_Bx16xSxS_0': fside_Bx16xSxS_0, 'mask_Bx1xSxS_bk0': mask_Bx1xSxS_bk0, 'L0_cond_Wi': _L0_cond_in['Wi'], 'L0_cond_bi': _L0_cond_in['bi'], 'L0_cond_Wo': _L0_cond_in['Wo'], 'L0_cond_bo': _L0_cond_in['bo'], 'L0_cond_gamma': _L0_cond_in['gamma'], 'L0_cond_beta': _L0_cond_in['beta'], 'L1_cond_W_ada': _L1_cond_in['W_ada'], 'L1_cond_b_ada': _L1_cond_in['b_ada'], 'L1_cond_Wq': _L1_cond_in['Wq'], 'L1_cond_bq': _L1_cond_in['bq'], 'L1_cond_Wk': _L1_cond_in['Wk'], 'L1_cond_bk': _L1_cond_in['bk'], 'L1_cond_Wv': _L1_cond_in['Wv'], 'L1_cond_bv': _L1_cond_in['bv'], 'L1_cond_Wo': _L1_cond_in['Wo'], 'L1_cond_bo': _L1_cond_in['bo'], 'L1_cond_W1': _L1_cond_in['W1'], 'L1_cond_b1': _L1_cond_in['b1'], 'L1_cond_W2': _L1_cond_in['W2'], 'L1_cond_b2': _L1_cond_in['b2'], 'L1_cond_g2': _L1_cond_in['g2'], 'L1_cond_beta2': _L1_cond_in['beta2']}

def reference(x, itok_B_0_7, itok_B_34_63, fside_Bx16xSxS_0, mask_Bx1xSxS_bk0, L0_cond_Wi, L0_cond_bi, L0_cond_Wo, L0_cond_bo, L0_cond_gamma, L0_cond_beta, L1_cond_W_ada, L1_cond_b_ada, L1_cond_Wq, L1_cond_bq, L1_cond_Wk, L1_cond_bk, L1_cond_Wv, L1_cond_bv, L1_cond_Wo, L1_cond_bo, L1_cond_W1, L1_cond_b1, L1_cond_W2, L1_cond_b2, L1_cond_g2, L1_cond_beta2):
    import jax
    import jax.numpy as jnp

    def _L0_cond_ref(input_tensor, expert_idx, Wi, bi, Wo, bo, gamma, beta):
        import jax, jax.numpy as jnp
        import numpy as np
        E, H, I = (8, 256, 1024)
        B, S = (4, 256)
        LN_EPS = 1e-12
        Wi_b = Wi[expert_idx]
        bi_b = bi[expert_idx]
        Wo_b = Wo[expert_idx]
        bo_b = bo[expert_idx]
        g_b = gamma[expert_idx]
        be_b = beta[expert_idx]
        h = jax.nn.gelu(jnp.einsum('bsh,bhi->bsi', input_tensor, Wi_b) + bi_b[:, None, :], approximate=False)
        o = jnp.einsum('bsi,bih->bsh', h, Wo_b) + bo_b[:, None, :]
        r = o + input_tensor
        mu = jnp.mean(r, axis=-1, keepdims=True)
        var = jnp.mean(jnp.square(r - mu), axis=-1, keepdims=True)
        y = (r - mu) * jax.lax.rsqrt(var + LN_EPS)
        return y * g_b[:, None, :] + be_b[:, None, :]

    def _L1_cond_ref(src, src_mask, timestep, attention_bias, W_ada, b_ada, Wq, bq, Wk, bk, Wv, bv, Wo, bo, W1, b1, W2, b2, g2, beta2):
        import jax, jax.numpy as jnp
        import numpy as np
        import math
        D_MODEL = 256
        N_HEAD = 16
        HEAD_DIM = D_MODEL // N_HEAD
        D_FF = 1024
        NUM_STEPS = 100.0
        RESCALE = 4000.0
        EPS = 1e-05

        def _sin_emb(t):
            half = D_MODEL // 2
            x = t.astype(jnp.float32) / NUM_STEPS * RESCALE
            freqs = jnp.exp(jnp.arange(half, dtype=jnp.float32) * (-math.log(10000.0) / (half - 1)))
            e = x[:, None] * freqs[None, :]
            return jnp.concatenate([jnp.sin(e), jnp.cos(e)], axis=-1)

        def _ln(x):
            m = jnp.mean(x, axis=-1, keepdims=True)
            v = jnp.var(x, axis=-1, keepdims=True)
            return (x - m) / jnp.sqrt(v + EPS)

        def _gelu2(x):
            return x * jax.nn.sigmoid(1.702 * x)
        B, S, D = src.shape
        emb = jax.nn.silu(_sin_emb(timestep)) @ W_ada + b_ada
        scale, shift = jnp.split(emb[:, None, :], 2, axis=-1)
        x = _ln(src) * (1.0 + scale) + shift
        q = (x @ Wq + bq).reshape(B, S, N_HEAD, HEAD_DIM).transpose(0, 2, 1, 3)
        k = (x @ Wk + bk).reshape(B, S, N_HEAD, HEAD_DIM).transpose(0, 2, 1, 3)
        v = (x @ Wv + bv).reshape(B, S, N_HEAD, HEAD_DIM).transpose(0, 2, 1, 3)
        scores = jnp.einsum('bhqd,bhkd->bhqk', q / math.sqrt(HEAD_DIM), k)
        scores = scores + attention_bias
        scores = jnp.where(src_mask, -jnp.inf, scores.astype(jnp.float32))
        probs = jax.nn.softmax(scores, axis=-1).astype(v.dtype)
        ctx = jnp.einsum('bhqk,bhkd->bhqd', probs, v)
        ctx = ctx.transpose(0, 2, 1, 3).reshape(B, S, D)
        x = x + (ctx @ Wo + bo)
        h = _ln(x) * g2 + beta2
        ff = _gelu2(h @ W1 + b1) @ W2 + b2
        return x + ff
    x = _L0_cond_ref(x, itok_B_0_7, L0_cond_Wi, L0_cond_bi, L0_cond_Wo, L0_cond_bo, L0_cond_gamma, L0_cond_beta)
    x = _L1_cond_ref(x, mask_Bx1xSxS_bk0, itok_B_34_63, fside_Bx16xSxS_0, L1_cond_W_ada, L1_cond_b_ada, L1_cond_Wq, L1_cond_bq, L1_cond_Wk, L1_cond_bk, L1_cond_Wv, L1_cond_bv, L1_cond_Wo, L1_cond_bo, L1_cond_W1, L1_cond_b1, L1_cond_W2, L1_cond_b2, L1_cond_g2, L1_cond_beta2)
    return x

_drawn_inputs = setup_inputs


def setup_inputs(seed=0):
    import zlib

    import numpy as np

    out = dict(_drawn_inputs(seed))
    spreads = {'L0_cond_bi': (0.0, 0.1),
     'L0_cond_bo': (0.0, 0.1),
     'L0_cond_gamma': (1.0, 0.2),
     'L0_cond_beta': (0.0, 0.1),
     'L1_cond_b_ada': (0.0, 0.1),
     'L1_cond_bq': (0.0, 0.8),
     'L1_cond_bk': (0.0, 0.8),
     'L1_cond_bv': (0.0, 0.267),
     'L1_cond_bo': (0.0, 0.1),
     'L1_cond_b1': (0.0, 0.1),
     'L1_cond_b2': (0.0, 0.1),
     'L1_cond_g2': (1.0, 0.6),
     'L1_cond_beta2': (0.0, 0.676)}
    factors = {'fside_Bx16xSxS_0': 8.0, 'L1_cond_Wq': 8.0, 'L1_cond_Wk': 8.0}
    for name, (base, spread) in spreads.items():
        noise = np.random.default_rng([zlib.crc32(name.encode()), seed]).standard_normal(out[name].shape)
        drawn = base * np.exp(spread * noise) if base else spread * noise
        out[name] = jnp.asarray(drawn.astype(out[name].dtype))
    for name, factor in factors.items():
        out[name] = (out[name] * factor).astype(out[name].dtype)
    return out
```

```python
from contextlib import ExitStack

import concourse.bass as bass
from concourse import mybir

F32 = mybir.dt.float32
F32R = mybir.dt.float32r
BF16 = mybir.dt.bfloat16
I32 = mybir.dt.int32
U8 = mybir.dt.uint8
ALU = mybir.AluOpType
ACT = mybir.ActivationFunctionType
AX = mybir.AxisListType

B, S, D, I, H, HD = 8, 512, 256, 1024, 16, 16
NT = S // 128
NK = D // 128
NM = I // 128
VW = HD + 1
NEG = -1.0e30
TERMS = [(0, 0), (0, 1), (1, 0), (1, 1), (0, 2), (2, 0), (1, 2), (2, 1)]


class Queue:

    def __init__(self, nc, ctx, name):
        self.nc, self.ctx, self.name = nc, ctx, name
        self.items = []
        self.phase()

    def phase(self):
        self.n = 0
        self.sem = self.ctx.enter_context(self.nc.semaphore(f"s_{self.name}{len(self.items)}"))

    def op(self, fn, *waits, inc=True):
        if inc:
            self.n += 1
        self.items.append((fn, [w for w in waits if w], (self.sem, 1) if inc else None))
        return (self.sem, self.n) if inc else None

    def dma(self, slot, out, in_, *waits, **kw):
        slot[1] += 16
        self.items.append((lambda e: e.dma_start(out, in_, **kw), [w for w in waits if w], (slot[0], 16)))
        return (slot[0], slot[1])

    def wait(self, *waits):
        self.items.append((None, [w for w in waits if w], None))

    def last(self):
        return (self.sem, self.n) if self.n else None

    def emit(self, eng):
        passed = {}
        for fn, waits, inc in self.items:
            for sem, v in waits:
                if passed.get(sem.name, 0) < v:
                    eng.wait_ge(sem, v)
                    passed[sem.name] = v
            if fn is None:
                continue
            ins = fn(eng)
            if inc:
                ins.then_inc(*inc)


def program(nc, x, itok, tstep, bias, mask, Wi, bi, Wo0, bo0, gam, bet, Wada, bada, Wq, bq, Wk, bk, Wv, bv,
            Wo, bo, W1, b1, W2, b2, g2, be2, ident, freqs, out):
    with ExitStack() as ctx:
        sp, pe, act, dve, pool = (Queue(nc, ctx, n) for n in ("sp", "pe", "act", "dve", "pool"))
        slots = []

        def slot(name):
            s = [ctx.enter_context(nc.semaphore(f"d_{name}")), 0]
            slots.append(s)
            return s

        def dram(name, shape, dt):
            return nc.dram_tensor(name, shape, dt, kind="Internal").ap()

        sc_qk = dram("sc_qk", [B, 2, 3, D, S], BF16)
        sc_v = dram("sc_v", [B, S, H * VW], F32)
        sc_x2 = dram("sc_x2", [B, S, D], F32)
        sc_c = dram("sc_c", [B, S, D], F32)

        def rows(a):
            return a.rearrange("(t p) d -> p t d", p=128)

        base = ctx.enter_context(ExitStack())

        def sbuf(stack, name, shape, dt=F32):
            return stack.enter_context(nc.sbuf_tensor(f"t_{name}", shape, dt))

        idf = sbuf(base, "idf", [128, 128])
        idb = sbuf(base, "idb", [128, 128], BF16)
        d_id = slot("id")
        t_idf = sp.dma(d_id, idf[:, :], ident)
        t_idb = dve.op(lambda e: e.tensor_copy(idb[:, :], idf[:, :]), t_idf)

        def barrier():
            ends = [q.last() for q in (pe, act, dve, pool)] + [(s[0], s[1]) for s in slots if s[1]]
            for q in (pe, act, dve, pool):
                q.phase()
            for q in (sp, pe, act, dve, pool):
                q.wait(*ends)

        def phase(body):
            with ExitStack() as st:
                body(st)

        def mm3(dst, pairs, *waits):
            todo = [(lh[a], rh[c]) for lh, rh in pairs for a, c in ((0, 0), (0, 1), (1, 0))]
            for n, (l, r) in enumerate(todo):
                end = n == len(todo) - 1
                t = pe.op(lambda e, l=l, r=r, n=n, end=end: e.matmul(dst, l, r, start=n == 0, stop=end),
                          *(waits if n == 0 else ()), inc=end)
            return t

        def rsqrt(v, y, a, hv, *waits):
            k = dve.op(lambda e: e.tensor_scalar(a.bitcast(I32), v.bitcast(I32), 1, None, ALU.arith_shift_right), *waits)
            t = dve.op(lambda e: e.tensor_scalar(hv, v, -0.5, None, ALU.mult), *waits)
            k = dve.op(lambda e: e.tensor_scalar(y.bitcast(I32), a.bitcast(I32), -1.0, 1597463007.0, ALU.mult, ALU.add), k)
            for _ in range(3):
                k = dve.op(lambda e: e.tensor_tensor(a, y, y, ALU.mult), k)
                k = dve.op(lambda e: e.tensor_tensor(a, a, hv, ALU.mult), k, t)
                k = dve.op(lambda e: e.scalar_tensor_tensor(out=y, in0=a, scalar=1.5, in1=y, op0=ALU.add, op1=ALU.mult), k)
            return k

        def layernorm(src, dst, st, mv, sm, eps, t_src, *free):
            ks = [dve.op(lambda e, t=t: e.bn_stats(st[:, t, :], src[:, t, :]), t_src) for t in range(NT)]
            ks = [dve.op(lambda e, t=t: e.bn_aggr(mv[:, t, :], st[:, t, :]), ks[t]) for t in range(NT)]
            k = dve.op(lambda e: e.tensor_scalar(sm[:, 0, :], mv[:, :, 1], eps, None, ALU.add), ks[-1])
            k = rsqrt(sm[:, 0, :], sm[:, 1, :], sm[:, 2, :], sm[:, 3, :], k)
            for t in range(NT):
                k2 = dve.op(lambda e, t=t: e.tensor_scalar(dst[:, t, :], src[:, t, :], mv[:, t, 0:1], sm[:, 1, t:t + 1],
                                                           ALU.subtract, ALU.mult), k, *free)
            return k2

        def bc(a, n):
            return a.unsqueeze(1).broadcast_to([128, n, D])

        @phase
        def _(st):
            def sb(name, shape, dt=F32):
                return sbuf(st, name, shape, dt)

            psX = st.enter_context(nc.psum_tensor("psX", [128, NK, 512], F32))
            psH = [st.enter_context(nc.psum_tensor(f"psH{i}", [128, 512], F32)) for i in range(2)]
            psO = st.enter_context(nc.psum_tensor("psO", [128, NT, D], F32))
            psQ = [st.enter_context(nc.psum_tensor(f"psQ{i}", [128, 512], F32)) for i in range(2)]

            itk = sb("itk", [1, B], I32)
            xs = [sb(f"x{i}", [128, NT, D]) for i in range(2)]
            wi_f, wo_f = sb("wi_f", [128, NK, I]), sb("wo_f", [128, NM, D])
            wi_s = [sb(f"wi{n}", [128, NK, I], F32R) for n in "hl"]
            wo_s = [sb(f"wo{n}", [128, NM, D], F32R) for n in "hl"]
            bis = [sb(f"bi{i}", [128, NM]) for i in range(2)]
            ob = [sb(f"ob{i}", [128, 3, D]) for i in range(2)]
            xT = [sb(f"xT{n}", [128, NK, S], F32R) for n in "hl"]
            hf = [sb(f"hf{i}", [128, S]) for i in range(3)]
            hT = [sb(f"hT{n}", [128, NM, S], F32R) for n in "hl"]
            xb, r1, y1 = (sb(n, [128, NT, D]) for n in ("xb", "r1", "y1"))
            x2 = [sb(f"x2{i}", [128, NT, D]) for i in range(2)]
            x2T = [sb(f"x2T{n}", [128, NK, S], F32R) for n in "hl"]
            qf, qr = sb("qf", [128, NK, S]), sb("qr", [128, NK, S])
            parts = [sb(f"parts{i}", [128, 3, NK, S], BF16) for i in range(2)]
            v17 = sb("v17", [128, NT, H, VW])
            ss = sb("ss", [128, B, 2 * D])
            wsm = {n: [sb(f"w{n}{p}", [128, NK, D], F32R) for p in "hl"] for n in "qkv"}
            bqk = sb("bqk", [128, 2, NK])
            bvb = sb("bvb", [128, D])
            stt, mv, sm = sb("stt", [128, NT, 6]), sb("mv", [128, NT, 2]), sb("sm", [128, 4, NT])

            d_c = slot("c")
            wstage = {"q": y1, "k": r1, "v": xb}
            t_c = sp.dma(d_c, itk[:, :], itok.rearrange("(a b) -> a b", a=1))
            tsb = sb("tsb", [128, B], I32)
            sp.dma(d_c, tsb[:, :], tstep.rearrange("(a b) -> a b", a=1).broadcast_to([128, B]))
            frq = sb("frq", [128, 1])
            sp.dma(d_c, frq[:, :], freqs)
            for n, w in (("q", Wq), ("k", Wk), ("v", Wv)):
                sp.dma(d_c, wstage[n][:, 0:NK, :], w.rearrange("(k p) n -> p k n", p=128))
            for n, a in ((0, bq), (1, bk)):
                sp.dma(d_c, bqk[:, n, :], a)
            sp.dma(d_c, bvb[:, :], bv.rearrange("(a n) -> a n", a=1).broadcast_to([128, D]))
            wad = qf
            bad = qr[:, 0, :]
            sp.dma(d_c, wad[:, :, :], Wada.rearrange("(k p) n -> p k n", p=128))
            t_c = sp.dma(d_c, bad, bada.rearrange("(a n) -> a n", a=1).broadcast_to([128, 2 * D]))
            d_x, d_wi, d_wo, d_s = [slot(f"x{i}") for i in range(2)], slot("wi"), slot("wo"), [slot(f"s{i}") for i in range(2)]
            expert = {}

            def load_x(b, *waits):
                return sp.dma(d_x[b % 2], xs[b % 2][:, :, :], rows(x[b]), *waits)

            def ix(b):
                return bass.ds(expert[b], 1)

            def dyn(sl, dst, src, *waits):
                sl[1] += 16
                sp.items.append((lambda e: e.dma_start(dst(), src()), [w for w in waits if w], (sl[0], 16)))
                return (sl[0], sl[1])

            def load_wi(b, *waits):
                return dyn(d_wi, lambda: wi_f[:, :, :], lambda: Wi[ix(b), :, :].rearrange("e (k p) i -> p (e k) i", p=128), *waits)

            def load_wo(b, *waits):
                return dyn(d_wo, lambda: wo_f[:, :, :], lambda: Wo0[ix(b), :, :].rearrange("e (m p) n -> p (e m) n", p=128), *waits)

            def load_small(b, *waits):
                sl, t = d_s[b % 2], ob[b % 2]
                dyn(sl, lambda: bis[b % 2][:, :], lambda: bi[ix(b), :, :].rearrange("e p m -> (e p) m"), *waits)
                for n, a in enumerate((bo0, gam, bet)):
                    k = dyn(sl, lambda n=n: t[:, n, :], lambda a=a: a[ix(b), :].broadcast_to([128, D]), *waits)
                return k

            def read_experts(e):
                for b in range(B):
                    expert[b] = e.value_load(itk[0:1, b:b + 1], min_val=0, max_val=7)

            sp.wait(t_c)
            sp.items.append((read_experts, [], None))
            t_x, t_wi, t_wo, t_sm = {0: load_x(0)}, {0: load_wi(0)}, {0: load_wo(0)}, {0: load_small(0)}
            t_x[1], t_sm[1] = load_x(1), load_small(1)

            em = sb("em", [128, 8, 2 * B])
            e_, n_, r_, w_ = (em[:, i, 0:B] for i in range(4))
            sc_ = [em[:, 4, 0:B], em[:, 4, B:2 * B]]
            k = dve.op(lambda e: e.tensor_copy(w_, tsb[:, :]), t_c)
            k = dve.op(lambda e: e.tensor_scalar(e_, w_, 0.01, None, ALU.mult), k)
            k = dve.op(lambda e: e.tensor_scalar(n_, e_, 4097.0, None, ALU.mult), k)
            k = dve.op(lambda e: e.tensor_tensor(r_, n_, e_, ALU.subtract), k)
            k = dve.op(lambda e: e.tensor_tensor(n_, n_, r_, ALU.subtract), k)
            k = dve.op(lambda e: e.tensor_tensor(r_, e_, n_, ALU.subtract), k)
            k = dve.op(lambda e: e.scalar_tensor_tensor(out=w_, in0=n_, scalar=-100.0, in1=w_, op0=ALU.mult, op1=ALU.add), k)
            k = dve.op(lambda e: e.scalar_tensor_tensor(out=w_, in0=r_, scalar=-100.0, in1=w_, op0=ALU.mult, op1=ALU.add), k)
            k = dve.op(lambda e: e.scalar_tensor_tensor(out=e_, in0=w_, scalar=0.01, in1=e_, op0=ALU.mult, op1=ALU.add), k)
            k = dve.op(lambda e: e.tensor_scalar(e_, e_, 4000.0, None, ALU.mult), k)
            k = dve.op(lambda e: e.tensor_scalar(e_, e_, frq[:, 0:1], None, ALU.mult), k)
            t_sin = []
            PI = 3.1415925
            for c in range(2):
                k = dve.op(lambda e, c=c: e.tensor_scalar(n_, e_, 0.15915494309189535, 0.25 * c, ALU.mult, ALU.add), k)
                k = dve.op(lambda e: e.tensor_scalar(n_, n_, 12582912.0, None, ALU.add), k)
                k = dve.op(lambda e: e.tensor_scalar(n_, n_, -12582912.0, None, ALU.add), k)
                k = dve.op(lambda e: e.scalar_tensor_tensor(out=r_, in0=n_, scalar=-6.28125, in1=e_, op0=ALU.mult, op1=ALU.add), k)
                k = dve.op(lambda e: e.scalar_tensor_tensor(out=r_, in0=n_, scalar=-0.0019350051879882812, in1=r_, op0=ALU.mult, op1=ALU.add), k)
                k = dve.op(lambda e: e.scalar_tensor_tensor(out=r_, in0=n_, scalar=-3.0199159819e-07, in1=r_, op0=ALU.mult, op1=ALU.add), k)
                if c:
                    k = dve.op(lambda e: e.tensor_scalar(r_, r_, 1.5707963267948966, None, ALU.add), k)
                k = dve.op(lambda e, c=c: e.tensor_scalar(sc_[c], r_, PI, -PI, ALU.min, ALU.max), k)
                t_sin.append(k)
            sn, ex = em[:, 5, :], em[:, 6, :]
            ta = act.op(lambda e: e.activation(sn, em[:, 4, :], ACT.Sin), *t_sin)
            ta2 = act.op(lambda e: e.activation(ex, sn, ACT.Exp, scale=-1.0), ta)
            k = dve.op(lambda e: e.tensor_scalar(ex, ex, 1.0, None, ALU.add), ta2)
            k = dve.op(lambda e: e.reciprocal(ex, ex), k)
            k = dve.op(lambda e: e.tensor_tensor(ex, ex, sn, ALU.mult), k)
            silb = [x2[i].rearrange("p t d -> p (t d)").rearrange("p (b m) -> p b m", m=128) for i in range(2)]
            for c in range(2):
                k2 = dve.op(lambda e, c=c: e.tensor_copy(silb[c], em[:, 6, c * B:(c + 1) * B].unsqueeze(2).broadcast_to([128, B, 128])), k)
            t_silb = k2
            t_bad = dve.op(lambda e: e.tensor_scalar(bad[:, 0:D], bad[:, 0:D], 1.0, None, ALU.add), t_c)
            t_ss = {}
            for b in range(B):
                for c in range(2):
                    t = pe.op(lambda e, b=b, c=c: e.matmul(psQ[b % 2][:, :], silb[c][:, b, :], wad[:, c, :], start=c == 0, stop=c == 1),
                              t_silb, t_c, t_ss.get(b - 2), inc=c == 1)
                t_ss[b] = dve.op(lambda e, b=b: e.tensor_tensor(ss[:, b, :], psQ[b % 2][:, :], bad, ALU.add), t, t_bad)
            t_emb = t_ss[B - 1]

            t_w = {}
            for n in "qkv":
                src, hl = wstage[n][:, 0:NK, :], wsm[n]
                k = act.op(lambda e, hl=hl, src=src: e.activation(hl[0][:, :, :], src, ACT.Copy), t_c)
                t_w[n] = pool.op(lambda e, hl=hl, src=src: e.tensor_tensor(hl[1][:, :, :], src, hl[0][:, :, :].bitcast(F32), ALU.subtract), k)
            t_bq = dve.op(lambda e: e.tensor_scalar(bqk[:, 0, :], bqk[:, 0, :], 0.25, None, ALU.mult), t_c)
            t_one = dve.op(lambda e: e.memset(v17[:, :, :, HD:VW], 1.0))

            tk = {}

            def split_wi(b, *free):
                k = act.op(lambda e: e.activation(wi_s[0][:, :, :], wi_f[:, :, :], ACT.Copy), t_wi[b], *free)
                tk["wi", b] = pool.op(lambda e: e.tensor_tensor(wi_s[1][:, :, :], wi_f[:, :, :], wi_s[0][:, :, :].bitcast(F32), ALU.subtract), k, *free)
                if b + 1 < B:
                    t_wi[b + 1] = load_wi(b + 1, tk["wi", b])

            def split_wo(b, *free):
                k = act.op(lambda e: e.activation(wo_s[0][:, :, :], wo_f[:, :, :], ACT.Copy), t_wo[b], *free)
                tk["wo", b] = pool.op(lambda e: e.tensor_tensor(wo_s[1][:, :, :], wo_f[:, :, :], wo_s[0][:, :, :].bitcast(F32), ALU.subtract), k, *free)
                if b + 1 < B:
                    t_wo[b + 1] = load_wo(b + 1, tk["wo", b])

            def turn(src, dst, t_src, psum_free, dst_free):
                for kk in range(NK):
                    for t in range(NT):
                        p = pe.op(lambda e, kk=kk, t=t: e.transpose(psX[:, kk, t * 128:(t + 1) * 128], src[:, t, kk * 128:(kk + 1) * 128], idf[:, :]),
                                  t_src, psum_free, t_idf, inc=(kk == NK - 1 and t == NT - 1))
                k = act.op(lambda e: e.activation(dst[0][:, :, :], psX[:, :, :], ACT.Copy), p, dst_free)
                return dve.op(lambda e: e.tensor_tensor(dst[1][:, :, :], psX[:, :, :], dst[0][:, :, :].bitcast(F32), ALU.subtract), k)

            def hidden(b):
                for m in range(NM):
                    ms = slice(m * 128, (m + 1) * 128)
                    p = mm3(psH[m % 2][:, :], [([w[:, kk, ms] for w in wi_s], [z[:, kk, :] for z in xT]) for kk in range(NK)],
                            tk["wi", b], tk["xT", b], tk.get("gelu_ps", {}).get(m % 2))
                    f = hf[m % 3]
                    g = act.op(lambda e, m=m, f=f, b=b: e.activation(f[:, :], psH[m % 2][:, :], ACT.Gelu, bias=bis[b % 2][:, m:m + 1]),
                               p, t_sm[b], tk.get(("hf", m % 3)))
                    tk.setdefault("gelu_ps", {})[m % 2] = g
                    k = dve.op(lambda e, m=m, f=f: e.tensor_copy(hT[0][:, m, :], f[:, :]), g, tk.get(("O", b - 1)))
                    k = dve.op(lambda e, m=m, f=f: e.tensor_tensor(hT[1][:, m, :], f[:, :], hT[0][:, m, :].bitcast(F32), ALU.subtract), k)
                    tk["hf", m % 3] = k
                tk["H", b] = p
                tk["gelu", b] = g
                tk["hT", b] = k

            def down(b):
                for t in range(NT):
                    ts = slice(t * 128, (t + 1) * 128)
                    p = mm3(psO[:, t, :], [([z[:, m, ts] for z in hT], [w[:, m, :] for w in wo_s]) for m in range(NM)],
                            tk["hT", b], tk["wo", b], tk.get(("r1", b - 1)))
                tk["O", b] = p

            def norms(b):
                o = ob[b % 2]
                k = pool.op(lambda e: e.tensor_tensor(xb[:, :, :], xs[b % 2][:, :, :], bc(o[:, 0, :], NT), ALU.add),
                            t_x[b], t_sm[b], tk.get(("r1", b - 1)), t_w["v"])
                k = dve.op(lambda e: e.tensor_tensor(r1[:, :, :], psO[:, :, :], xb[:, :, :], ALU.add), k, tk["O", b], t_w["k"])
                tk["r1", b] = k
                k = layernorm(r1, y1, stt, mv, sm, 1e-12, k, t_w["q"], tk.get(("z", b - 1)))
                k = pool.op(lambda e: e.tensor_tensor(y1[:, :, :], y1[:, :, :], bc(o[:, 1, :], NT), ALU.mult), k)
                k = pool.op(lambda e: e.tensor_tensor(y1[:, :, :], y1[:, :, :], bc(o[:, 2, :], NT), ALU.add), k)
                tk["small", b] = k
                z = x2[b % 2]
                k = layernorm(y1, z, stt, mv, sm, 1e-5, k, tk.get(("x2T", b - 2)), tk.get(("sx2", b - 2)), t_emb)
                tk["z", b] = k
                k = pool.op(lambda e: e.tensor_tensor(z[:, :, :], z[:, :, :], bc(ss[:, b, 0:D], NT), ALU.mult), k, t_emb)
                k = pool.op(lambda e: e.tensor_tensor(z[:, :, :], z[:, :, :], bc(ss[:, b, D:2 * D], NT), ALU.add), k)
                tk["x2", b] = k

            d_p, d_v, d_x2 = [slot(f"p{i}") for i in range(2)], slot("v"), [slot(f"x2{i}") for i in range(2)]

            def qkv(b):
                tk["x2T", b] = turn(x2[b % 2], x2T, tk["x2", b], tk["xT", b + 1] if b + 1 < B else tk["xT", b], tk.get(("V", b - 1)))
                for n, (w, scale) in enumerate((("q", 0.25), ("k", 1.0))):
                    for mt in range(NK):
                        ms = slice(mt * 128, (mt + 1) * 128)
                        p = mm3(psQ[mt][:, :], [([u[:, kk, ms] for u in wsm[w]], [z[:, kk, :] for z in x2T]) for kk in range(NK)],
                                t_w[w], tk["x2T", b], tk.get(("psQ", mt)), t_emb)
                        k = act.op(lambda e, mt=mt, n=n, scale=scale: e.activation(qf[:, mt, :], psQ[mt][:, :], ACT.Identity,
                                                                                   bias=bqk[:, n, mt:mt + 1], scale=scale),
                                   p, t_bq, tk.get("qf"))
                        tk["psQ", mt] = k
                    pt, free = parts[n], tk.get(("parts", n))
                    k = dve.op(lambda e, pt=pt: e.tensor_copy(pt[:, 0, :, :], qf[:, :, :]), k, free)
                    k = pool.op(lambda e, pt=pt: e.tensor_tensor(qr[:, :, :], qf[:, :, :], pt[:, 0, :, :], ALU.subtract), k, tk.get("qr"))
                    tk["qf"] = k
                    k = dve.op(lambda e, pt=pt: e.tensor_copy(pt[:, 1, :, :], qr[:, :, :]), k)
                    k = pool.op(lambda e, pt=pt: e.tensor_tensor(pt[:, 2, :, :], qr[:, :, :], pt[:, 1, :, :], ALU.subtract), k)
                    tk["qr"] = k
                    for c in range(3):
                        tk["parts", n] = sp.dma(d_p[n], sc_qk[b, n, c].rearrange("(k p) s -> p k s", p=128), pt[:, c, :, :], k)
                for half in range(2):
                    for t in (2 * half, 2 * half + 1):
                        ts = slice(t * 128, (t + 1) * 128)
                        p = mm3(psQ[half][:, (t % 2) * D:(t % 2 + 1) * D],
                                [([z[:, kk, ts] for z in x2T], [u[:, kk, :] for u in wsm["v"]]) for kk in range(NK)],
                                t_w["v"], tk.get(("psQ", half)))
                    for t in (2 * half, 2 * half + 1):
                        k = dve.op(lambda e, t=t, half=half: e.tensor_tensor(
                            v17[:, t, :, 0:HD], psQ[half][:, (t % 2) * D:(t % 2 + 1) * D].rearrange("p (h d) -> p h d", d=HD),
                            bvb[:, :].rearrange("p (h d) -> p h d", d=HD), ALU.add), p, tk.get("sv"), t_c)
                    tk["psQ", half] = k
                tk["V", b] = p
                tk["sv"] = sp.dma(d_v, rows(sc_v[b]), v17[:, :, :, :].rearrange("p t h v -> p t (h v)"), k, t_one)
                tk["sx2", b] = sp.dma(d_x2[b % 2], rows(sc_x2[b]), x2[b % 2][:, :, :], tk["x2", b])

            split_wi(0)
            split_wo(0)
            for i in range(B + 1):
                if i < B:
                    tk["xT", i] = turn(xs[i % 2], xT, t_x[i], tk.get(("x2T", i - 2)), tk.get(("H", i - 1)))
                    hidden(i)
                    down(i)
                    if i + 1 < B:
                        split_wi(i + 1, tk["H", i])
                    norms(i)
                    if i + 1 < B:
                        split_wo(i + 1, tk["O", i])
                if i >= 1:
                    qkv(i - 1)
                if i + 2 < B:
                    t_x[i + 2] = load_x(i + 2, tk["xT", i], tk["r1", i])
                    t_sm[i + 2] = load_small(i + 2, tk["gelu", i], tk["small", i])
        barrier()

        @phase
        def _(st):
            def sb(name, shape, dt=F32):
                return sbuf(st, name, shape, dt)

            NB, NP = 6, 6
            psS = [st.enter_context(nc.psum_tensor(f"psS{i}", [128, 512], F32)) for i in range(2)]
            psT = [st.enter_context(nc.psum_tensor(f"psT{i}", [128, 2, NT, 128], F32)) for i in range(2)]
            psV = st.enter_context(nc.psum_tensor("psV", [128, 512], F32))
            psC = st.enter_context(nc.psum_tensor("psC", [128, NT, 4, 32], F32))

            bt = [sb(f"bt{i}", [128, NT, S]) for i in range(NB)]
            pt = [sb(f"pt{i}", [128, NT, S]) for i in range(NP)]
            qs = [sb(f"qs{i}", [128, 8, S], BF16) for i in range(2)]
            ks = [sb(f"ks{i}", [128, 8, S], BF16) for i in range(2)]
            vs = [sb(f"vs{i}", [128, NT, H, VW]) for i in range(2)]
            mk = [sb(f"mk{i}", [128, NT, S], U8) for i in range(2)]
            mb = [sb(f"mb{i}", [128, NT, S], BF16) for i in range(2)]
            na = [sb(f"na{i}", [128, NT]) for i in range(2)]
            nm = sb("nm", [128, 8])
            cv = sb("cv", [128, 512])
            den = sb("den", [128, NT, 4])
            cx = [sb(f"cx{i}", [128, NT, D]) for i in range(2)]
            d_b = [slot(f"b{i}") for i in range(NB)]
            d_q = [slot(f"q{i}") for i in range(2)]
            d_m = [slot(f"m{i}") for i in range(2)]
            d_o = [slot(f"o{i}") for i in range(2)]
            N = B * H * NT
            tk = {}
            t_vz = dve.op(lambda e: e.memset(psV[:, :], 0.0))

            def load_qk(n):
                b, half = divmod(n, 2)
                free = tk.get(("QK", 32 * (n - 1) - 1))
                for dst, w in ((qs, 0), (ks, 1)):
                    for i, c in enumerate(TERMS):
                        src = sc_qk[b, w, c[w]].rearrange("(h d) s -> d h s", d=HD)[:, 8 * half:8 * half + 8, :]
                        tk["qs", n] = sp.dma(d_q[n % 2], dst[n % 2][i * HD:(i + 1) * HD, :, :], src, free)

            def load_batch(b):
                free = [tk.get(("PV", 4 * (b - 1) - 1)), tk.get(("mb", b - 2)), tk.get(("na", b - 2))]
                sp.dma(d_m[b % 2], vs[b % 2][:, :, :, :].rearrange("p t h v -> p t (h v)"), rows(sc_v[b]), *free)
                t = tk["vm", b] = sp.dma(d_m[b % 2], mk[b % 2][:, :, :], rows(mask[b]), *free)
                k = dve.op(lambda e: e.tensor_reduce(na[b % 2][:, :], mk[b % 2][:, :, :], AX.X, ALU.min), t, tk.get(("C", 4 * (b - 1) - 1)))
                tk["na", b] = dve.op(lambda e: e.tensor_scalar(na[b % 2][:, :], na[b % 2][:, :], -1.0, 1.0, ALU.mult, ALU.add), k)
                tk["mb", b] = pool.op(lambda e: e.tensor_scalar(mb[b % 2][:, :, :], mk[b % 2][:, :, :], NEG, None, ALU.mult),
                                      t, tk.get(("QK", 64 * (b - 1) - 1)))

            def load_bias(u):
                tk["bt", u] = sp.dma(d_b[u % NB], bt[u % NB][:, :, :], rows(bias[u // H, u % H]), tk.get(("T", 4 * (u - NB) + 3)))

            def scores(n):
                u, t = divmod(n, NT)
                b, h = divmod(u, H)
                g = u // 8 % 2
                ts = slice(t * 128, (t + 1) * 128)
                pe.op(lambda e: e.matmul(psS[n % 2][:, :], idb[:, :], mb[b % 2][:, t, :], start=True, stop=False),
                      tk["mb", b], tk.get(("max", n - 2)), t_idb, inc=False)
                tk["QK", n] = pe.op(lambda e: e.matmul(psS[n % 2][:, :], qs[g][:, h % 8, ts], ks[g][:, h % 8, :], start=False, stop=True),
                                    tk["qs", u // 8])
                s = bt[u % NB][:, t, :]
                tk["max", n] = dve.op(lambda e: e.tensor_tensor_reduce(s, psS[n % 2][:, :], s, -1.0, 3.0e38, ALU.add, ALU.min,
                                                                       nm[:, n % 8:n % 8 + 1]),
                                      tk["QK", n], tk["bt", u], tk.get(("exp", n - 8)))
                tk["exp", n] = act.op(lambda e: e.activation(s, s, ACT.Exp, bias=nm[:, n % 8:n % 8 + 1], scale=-1.0), tk["max", n])

            def turn_p(n):
                u, t = divmod(n, NT)
                j = n // 2
                for kk in range(NT):
                    tk["T", n] = pe.op(lambda e, kk=kk: e.transpose(psT[j % 2][:, n % 2, kk, :], bt[u % NB][:, t, kk * 128:(kk + 1) * 128], idf[:, :]),
                                       tk["exp", n], tk.get(("E", j - 2)), inc=kk == NT - 1)

            def evac(j):
                u, t = divmod(2 * j, NT)
                q = act if j % 5 in (0, 2, 4) else dve
                dst = pt[u % NP][:, :, t * 128:(t + 2) * 128].rearrange("p k (a q) -> p a k q", a=2)
                src = psT[j % 2][:, :, :, :]
                if q is act:
                    f = lambda e: e.activation(dst, src, ACT.Copy)
                else:
                    f = lambda e: e.tensor_copy(dst, src)
                tk["E", j] = q.op(f, tk["T", 2 * j + 1], tk.get(("PV", u // 4 - 1 if u % 4 >= NP - 4 else u // 4 - 2)) if u >= NP else None)
                tk["Es", u] = tk.get(("Es", u), []) + [tk["E", j]]

            def context(gi):
                b, hg = divmod(gi, 4)
                for kk in range(NT):
                    for g in range(4):
                        u = 4 * gi + g
                        tk["PV", gi] = pe.op(lambda e, kk=kk, g=g, u=u: e.matmul(
                            psV[32 * g:32 * g + VW, :], vs[b % 2][:, kk, u % H, :], pt[u % NP][:, kk, :],
                            start=kk == 0, stop=kk == NT - 1),
                            *tk["Es", u], tk["vm", b], tk.get(("cv", gi - 1)), t_vz, inc=(kk == NT - 1 and g == 3))
                tk["cv", gi] = act.op(lambda e: e.activation(cv[:, :], psV[:, :], ACT.Copy), tk["PV", gi], tk.get(("CT", gi - 1)))

            def finish(gi):
                b, hg = divmod(gi, 4)
                for t in range(NT):
                    p = pe.op(lambda e, t=t: e.transpose(psC[:, t, :, :].rearrange("p a c -> p (a c)"), cv[:, t * 128:(t + 1) * 128], idf[:, :]),
                              tk["cv", gi], tk.get(("C", gi - 1)), inc=t == NT - 1)
                tk["CT", gi] = p
                nb = na[b % 2][:, :].unsqueeze(2).broadcast_to([128, NT, 4])
                k = dve.op(lambda e: e.tensor_tensor(den[:, :, :], psC[:, :, :, HD], nb, ALU.mult), p, tk["na", b], tk.get(("C", gi - 1)))
                k = dve.op(lambda e: e.reciprocal(den[:, :, :], den[:, :, :]), k)
                k = dve.op(lambda e: e.tensor_tensor(den[:, :, :], den[:, :, :], nb, ALU.mult), k)
                dst = cx[b % 2][:, :, 64 * hg:64 * hg + 64].rearrange("p t (g d) -> p t g d", d=HD)
                tk["C", gi] = dve.op(lambda e: e.tensor_tensor(dst, psC[:, :, :, 0:HD], den[:, :, :].unsqueeze(3).broadcast_to([128, NT, 4, HD]), ALU.mult),
                                     k, tk.get(("so", b - 2)))
                if hg == 3:
                    tk["so", b] = sp.dma(d_o[b % 2], rows(sc_c[b]), cx[b % 2][:, :, :], tk["C", gi])

            load_batch(0)
            load_qk(0)
            LAG = 3
            nextb = 0
            for n in range(N + 40):
                while nextb < min(B * H, n // NT + NB) and (nextb < NB or ("T", 4 * (nextb - NB) + 3) in tk):
                    load_bias(nextb)
                    nextb += 1
                if n < N and n % 32 == 4 and n // 32 + 1 < 2 * B:
                    load_qk(n // 32 + 1)
                if n < N and n % 64 == 36 and n // 64 + 1 < B:
                    load_batch(n // 64 + 1)
                if n < N:
                    scores(n)
                m = n - LAG
                if 0 <= m < N:
                    turn_p(m)
                    if m % 2:
                        evac(m // 2)
                m = n - LAG - 2
                if 0 <= m < N and m % 16 == 15:
                    context(m // 16)
                m = n - LAG - 4
                if 0 <= m < N and m % 16 == 15:
                    finish(m // 16)
        barrier()

        @phase
        def _(st):
            def sb(name, shape, dt=F32):
                return sbuf(st, name, shape, dt)

            psX = st.enter_context(nc.psum_tensor("psX2", [128, NK, 512], F32))
            psH = [st.enter_context(nc.psum_tensor(f"psH2{i}", [128, 512], F32)) for i in range(2)]
            psO = st.enter_context(nc.psum_tensor("psO2", [128, NT, D], F32))
            psA = st.enter_context(nc.psum_tensor("psA2", [128, NT, D], F32))
            cs = [sb(f"cc{i}", [128, NT, D]) for i in range(2)]
            xs = [sb(f"cx2{i}", [128, NT, D]) for i in range(2)]
            x3 = [sb(f"x3{i}", [128, NT, D]) for i in range(2)]
            hl = [sb(f"hl{i}", [128, NT, D]) for i in range(2)]
            os_ = [sb(f"os{i}", [128, NT, D]) for i in range(2)]
            cT = [sb(f"cT{n}", [128, NK, S], F32R) for n in "hl"]
            lT = [sb(f"lT{n}", [128, NK, S], F32R) for n in "hl"]
            hf = [sb(f"chf{i}", [128, S]) for i in range(3)]
            hT = [sb(f"chT{n}", [128, NM, S], F32R) for n in "hl"]
            ws = {"o": (Wo, NK, D), "1": (W1, NK, I), "2": (W2, NM, D)}
            wf = {n: sb(f"cwf{n}", [128, k, w]) for n, (_, k, w) in ws.items()}
            wl = {n: [sb(f"cw{n}{p}", [128, k, w], F32R) for p in "hl"] for n, (_, k, w) in ws.items()}
            b1c = sb("b1c", [128, NM])
            rb = sb("rb", [128, 4, D])
            stt, mv, sm = sb("cstt", [128, NT, 6]), sb("cmv", [128, NT, 2]), sb("csm", [128, 4, NT])
            d_c = slot("cc")
            for n, (w, k, wd) in ws.items():
                sp.dma(d_c, wf[n][:, :, :], w.rearrange("(k p) n -> p k n", p=128))
            sp.dma(d_c, b1c[:, :], b1)
            for n, a in enumerate((bo, g2, be2, b2)):
                t_c = sp.dma(d_c, rb[:, n, :], a.rearrange("(a n) -> a n", a=1).broadcast_to([128, D]))
            d_l, d_out = [slot(f"cl{i}") for i in range(2)], [slot(f"out{i}") for i in range(2)]
            tk, t_w = {}, {}

            def load(b, *waits):
                sp.dma(d_l[b % 2], cs[b % 2][:, :, :], rows(sc_c[b]), *waits)
                tk["ld", b] = sp.dma(d_l[b % 2], xs[b % 2][:, :, :], rows(sc_x2[b]), *waits)

            load(0)
            load(1)
            for n in ws:
                k = act.op(lambda e, n=n: e.activation(wl[n][0][:, :, :], wf[n][:, :, :], ACT.Copy), t_c)
                t_w[n] = dve.op(lambda e, n=n: e.tensor_tensor(wl[n][1][:, :, :], wf[n][:, :, :], wl[n][0][:, :, :].bitcast(F32), ALU.subtract), k)

            def turn(src, dst, t_src, dst_free):
                for kk in range(NK):
                    for t in range(NT):
                        p = pe.op(lambda e, kk=kk, t=t: e.transpose(psX[:, kk, t * 128:(t + 1) * 128], src[:, t, kk * 128:(kk + 1) * 128], idf[:, :]),
                                  t_src, tk.get("psX"), inc=(kk == NK - 1 and t == NT - 1))
                k = act.op(lambda e: e.activation(dst[0][:, :, :], psX[:, :, :], ACT.Copy), p, dst_free)
                k = dve.op(lambda e: e.tensor_tensor(dst[1][:, :, :], psX[:, :, :], dst[0][:, :, :].bitcast(F32), ALU.subtract), k)
                tk["psX"] = k
                return k

            def attend(b):
                tk["cT", b] = turn(cs[b % 2], cT, tk["ld", b], tk.get(("A", b - 1)))
                for t in range(NT):
                    ts = slice(t * 128, (t + 1) * 128)
                    p = mm3(psA[:, t, :], [([z[:, kk, ts] for z in cT], [u[:, kk, :] for u in wl["o"]]) for kk in range(NK)],
                            tk["cT", b], t_w["o"], tk.get(("x3", b - 1)))
                tk["A", b] = p
                k = pool.op(lambda e: e.tensor_tensor(xs[b % 2][:, :, :], xs[b % 2][:, :, :], bc(rb[:, 0, :], NT), ALU.add), tk["ld", b], t_c)
                k = dve.op(lambda e: e.tensor_tensor(x3[b % 2][:, :, :], psA[:, :, :], xs[b % 2][:, :, :], ALU.add), k, p, tk.get(("out", b - 2)))
                tk["x3", b] = k
                h = hl[b % 2]
                k = layernorm(x3[b % 2], h, stt, mv, sm, 1e-5, k, tk.get(("lT", b - 2)))
                tk["ln", b] = k
                k = pool.op(lambda e: e.tensor_tensor(h[:, :, :], h[:, :, :], bc(rb[:, 1, :], NT), ALU.mult), k)
                tk["h", b] = pool.op(lambda e: e.tensor_tensor(h[:, :, :], h[:, :, :], bc(rb[:, 2, :], NT), ALU.add), k)
                tk["x3b", b] = pool.op(lambda e: e.tensor_tensor(x3[b % 2][:, :, :], x3[b % 2][:, :, :], bc(rb[:, 3, :], NT), ALU.add), tk["ln", b])
                if b + 2 < B:
                    load(b + 2, tk["cT", b], tk["x3", b])

            def ffn(b):
                tk["lT", b] = turn(hl[b % 2], lT, tk["h", b], tk.get(("H", b - 1)))
                for m in range(NM):
                    ms = slice(m * 128, (m + 1) * 128)
                    p = mm3(psH[m % 2][:, :], [([w[:, kk, ms] for w in wl["1"]], [z[:, kk, :] for z in lT]) for kk in range(NK)],
                            t_w["1"], tk["lT", b], tk.get(("g", m % 2)))
                    f = hf[m % 3]
                    g = act.op(lambda e, m=m, f=f: e.activation(f[:, :], psH[m % 2][:, :], ACT.Gelu_apprx_sigmoid, bias=b1c[:, m:m + 1]),
                               p, t_c, tk.get(("hf", m % 3)))
                    tk["g", m % 2] = g
                    k = dve.op(lambda e, m=m, f=f: e.tensor_copy(hT[0][:, m, :], f[:, :]), g, tk.get(("O", b - 1)))
                    k = dve.op(lambda e, m=m, f=f: e.tensor_tensor(hT[1][:, m, :], f[:, :], hT[0][:, m, :].bitcast(F32), ALU.subtract), k)
                    tk["hf", m % 3] = k
                tk["H", b] = p
                for t in range(NT):
                    ts = slice(t * 128, (t + 1) * 128)
                    p = mm3(psO[:, t, :], [([z[:, m, ts] for z in hT], [w[:, m, :] for w in wl["2"]]) for m in range(NM)],
                            k, t_w["2"], tk.get(("out", b - 1)))
                tk["O", b] = p

            def store(b):
                k = dve.op(lambda e: e.tensor_tensor(os_[b % 2][:, :, :], psO[:, :, :], x3[b % 2][:, :, :], ALU.add),
                           tk["O", b], tk["x3b", b], tk.get(("so", b - 2)))
                tk["out", b] = k
                tk["so", b] = sp.dma(d_out[b % 2], rows(out[b]), os_[b % 2][:, :, :], k)

            attend(0)
            for b in range(B):
                if b + 1 < B:
                    attend(b + 1)
                ffn(b)
                store(b)
        sp.wait(*[(s[0], s[1]) for s in slots if s[1]])

        block = ctx.enter_context(nc.Block())

        @block.sync
        def _(e):
            sp.emit(e)

        @block.tensor
        def _(e):
            pe.emit(e)

        @block.scalar
        def _(e):
            act.emit(e)

        @block.vector
        def _(e):
            dve.emit(e)

        @block.gpsimd
        def _(e):
            pool.emit(e)


_INS = ["x", "itok_B_0_7", "itok_B_34_63", "fside_Bx16xSxS_0", "mask_Bx1xSxS_bk0",
        "L0_cond_Wi", "L0_cond_bi", "L0_cond_Wo", "L0_cond_bo", "L0_cond_gamma", "L0_cond_beta",
        "L1_cond_W_ada", "L1_cond_b_ada", "L1_cond_Wq", "L1_cond_bq", "L1_cond_Wk", "L1_cond_bk",
        "L1_cond_Wv", "L1_cond_bv", "L1_cond_Wo", "L1_cond_bo", "L1_cond_W1", "L1_cond_b1",
        "L1_cond_W2", "L1_cond_b2", "L1_cond_g2", "L1_cond_beta2"]
_COLS = ["L0_cond_bi", "L1_cond_bq", "L1_cond_bk", "L1_cond_b1"]


def kernel(**inputs):
    import numpy as np
    import concourse.bacc as bacc
    from concourse.bass_utils import run_bass_kernel_spmd as run

    nc = bacc.Bacc("TRN2", target_bir_lowering=False, num_devices=1)
    arrays, args = {}, []

    def give(name, a):
        arrays[name] = a
        args.append(nc.dram_tensor(name, a.shape, mybir.dt.from_np(a.dtype), kind="ExternalInput").ap())

    for name in _INS:
        a = np.ascontiguousarray(inputs[name])
        if name.startswith("mask"):
            a = a.reshape(B, S, S)
        if name in _COLS:
            a = np.ascontiguousarray(np.swapaxes(a.reshape(a.shape[:-1] + (-1, 128)), -1, -2))
        give(f"in_{name}", a)
    give("ident", np.eye(128, dtype=np.float32))
    step = np.float32(-np.log(10000.0) / 127)
    give("freqs", np.exp(np.arange(128, dtype=np.float32) * step).astype(np.float32).reshape(128, 1))
    args.append(nc.dram_tensor("out_0", (B, S, D), F32, kind="ExternalOutput").ap())
    program(nc, *args)
    r = run(nc, [arrays], core_ids=[0])
    return r.results[0]["out_0"]
```

```python
from contextlib import ExitStack

import concourse.bass as bass
from concourse import mybir

F32 = mybir.dt.float32
F32R = mybir.dt.float32r
BF16 = mybir.dt.bfloat16
I32 = mybir.dt.int32
U8 = mybir.dt.uint8
ALU = mybir.AluOpType
ACT = mybir.ActivationFunctionType
AX = mybir.AxisListType

B, S, D, I, H, HD = 8, 512, 256, 1024, 16, 16
NT = S // 128
NK = D // 128
NM = I // 128
VW = HD + 1
NEG = -1.0e30
TERMS = [(0, 0), (0, 1), (1, 0), (1, 1), (0, 2), (2, 0)]
KR = HD * len(TERMS)


class Queue:

    def __init__(self, nc, ctx, name):
        self.nc, self.ctx, self.name = nc, ctx, name
        self.items = []
        self.phase()

    def phase(self):
        self.n = 0
        self.sem = self.ctx.enter_context(self.nc.semaphore(f"s_{self.name}{len(self.items)}"))

    def op(self, fn, *waits, inc=True):
        if inc:
            self.n += 1
        self.items.append((fn, [w for w in waits if w], (self.sem, 1) if inc else None))
        return (self.sem, self.n) if inc else None

    def dma(self, slot, out, in_, *waits, **kw):
        slot[1] += 16
        self.items.append((lambda e: e.dma_start(out, in_, **kw), [w for w in waits if w], (slot[0], 16)))
        return (slot[0], slot[1])

    def wait(self, *waits):
        self.items.append((None, [w for w in waits if w], None))

    def last(self):
        return (self.sem, self.n) if self.n else None

    def emit(self, eng):
        passed = {}
        for fn, waits, inc in self.items:
            for sem, v in waits:
                if passed.get(sem.name, 0) < v:
                    eng.wait_ge(sem, v)
                    passed[sem.name] = v
            if fn is None:
                continue
            ins = fn(eng)
            if inc:
                ins.then_inc(*inc)


def program(nc, x, x_t, itok, tstep, bias, mask, Wi, bi, Wo0, bo0, gam, bet, Wada, bada, Wq, bq, Wk, bk, Wv, bv,
            Wo, bo, W1, b1, W2, b2, g2, be2, ident, freqs, out):
    with ExitStack() as ctx:
        sp, pe, act, dve, pool = (Queue(nc, ctx, n) for n in ("sp", "pe", "act", "dve", "pool"))
        slots = []

        def slot(name):
            s = [ctx.enter_context(nc.semaphore(f"d_{name}")), 0]
            slots.append(s)
            return s

        def dram(name, shape, dt):
            return nc.dram_tensor(name, shape, dt, kind="Internal").ap()

        sc_qk = dram("sc_qk", [B, 2, 3, D, S], BF16)
        sc_v = dram("sc_v", [B, S, H * VW], F32)
        sc_x2 = dram("sc_x2", [B, S, D], F32)
        sc_ss = dram("sc_ss", [B, 2 * D], F32)
        sc_c = dram("sc_c", [B, S, D], F32)

        t_b = {}

        def rows(a):
            return a.rearrange("(t p) d -> p t d", p=128)

        base = ctx.enter_context(ExitStack())

        def sbuf(stack, name, shape, dt=F32):
            return stack.enter_context(nc.sbuf_tensor(f"t_{name}", shape, dt))

        idf = sbuf(base, "idf", [128, 128])
        idb = sbuf(base, "idb", [128, 128], BF16)
        d_id = slot("id")
        t_idf = sp.dma(d_id, idf[:, :], ident)
        t_idb = dve.op(lambda e: e.tensor_copy(idb[:, :], idf[:, :]), t_idf)

        def barrier():
            ends = [q.last() for q in (pe, act, dve, pool)] + [(s[0], s[1]) for s in slots if s[1]]
            for q in (pe, act, dve, pool):
                q.phase()
            for q in (sp, pe, act, dve, pool):
                q.wait(*ends)

        def phase(body):
            with ExitStack() as st:
                body(st)

        def mm3(dst, pairs, *waits):
            todo = [(lh[a], rh[c]) for lh, rh in pairs for a, c in ((0, 0), (0, 1), (1, 0))]
            for n, (l, r) in enumerate(todo):
                end = n == len(todo) - 1
                t = pe.op(lambda e, l=l, r=r, n=n, end=end: e.matmul(dst, l, r, start=n == 0, stop=end),
                          *(waits if n == 0 else ()), inc=end)
            return t

        def rsqrt(v, y, a, hv, *waits):
            k = dve.op(lambda e: e.tensor_scalar(a.bitcast(I32), v.bitcast(I32), 1, None, ALU.arith_shift_right), *waits)
            t = dve.op(lambda e: e.tensor_scalar(hv, v, -0.5, None, ALU.mult), *waits)
            k = dve.op(lambda e: e.tensor_scalar(y.bitcast(I32), a.bitcast(I32), -1.0, 1597463007.0, ALU.mult, ALU.add), k)
            for _ in range(3):
                k = dve.op(lambda e: e.tensor_tensor(a, y, y, ALU.mult), k)
                k = dve.op(lambda e: e.tensor_tensor(a, a, hv, ALU.mult), k, t)
                k = dve.op(lambda e: e.scalar_tensor_tensor(out=y, in0=a, scalar=1.5, in1=y, op0=ALU.add, op1=ALU.mult), k)
                yield
            return k

        def layernorm(src, dst, st, mv, sm, eps, t_src, *free):
            ks = []
            for t in range(NT):
                ks.append(dve.op(lambda e, t=t: e.bn_stats(st[:, t, :], src[:, t, :]), t_src))
                yield
            ks = [dve.op(lambda e, t=t: e.bn_aggr(mv[:, t, :], st[:, t, :]), ks[t]) for t in range(NT)]
            yield
            k = dve.op(lambda e: e.tensor_scalar(sm[:, 0, :], mv[:, :, 1], eps, None, ALU.add), ks[-1])
            k = yield from rsqrt(sm[:, 0, :], sm[:, 1, :], sm[:, 2, :], sm[:, 3, :], k)
            for t in range(NT):
                k2 = dve.op(lambda e, t=t: e.tensor_scalar(dst[:, t, :], src[:, t, :], mv[:, t, 0:1], sm[:, 1, t:t + 1],
                                                           ALU.subtract, ALU.mult), k, *free)
                yield
            return k2

        def advance(steps, n):
            for _ in range(n):
                if next(steps, self_end) is self_end:
                    return

        self_end = object()

        def bc(a, n):
            return a.unsqueeze(1).broadcast_to([128, n, D])

        @phase
        def _(st):
            def sb(name, shape, dt=F32):
                return sbuf(st, name, shape, dt)

            psX = st.enter_context(nc.psum_tensor("psX", [128, NK, 512], F32))
            psH = [st.enter_context(nc.psum_tensor(f"psH{i}", [128, 512], F32)) for i in range(2)]
            psO = st.enter_context(nc.psum_tensor("psO", [128, NT, D], F32))
            psQ = [st.enter_context(nc.psum_tensor(f"psQ{i}", [128, 512], F32)) for i in range(2)]

            wi_f, wo_f = sb("wi_f", [128, NK, I]), sb("wo_f", [128, NM, D])
            wi_s = [sb(f"wi{n}", [128, NK, I], F32R) for n in "hl"]
            wo_s = [sb(f"wo{n}", [128, NM, D], F32R) for n in "hl"]
            hT = [sb(f"hT{n}", [128, NM, S], F32R) for n in "hl"]
            xt = sb("xt", [128, NK, S])
            xT = [sb(f"xT{n}", [128, NK, S], F32R) for n in "hl"]
            hf = [sb(f"hf{i}", [128, S]) for i in range(3)]
            xs = [sb(f"x{i}", [128, NT, D]) for i in range(2)]
            bis = [sb(f"bi{i}", [128, NM]) for i in range(2)]
            ob = [sb(f"ob{i}", [128, 3, D]) for i in range(2)]
            xb = [sb(f"xb{i}", [128, NT, D]) for i in range(2)]
            r1, y1 = (sb(n, [128, NT, D]) for n in ("r1", "y1"))
            x2T = [sb(f"x2T{n}", [128, NK, S], F32R) for n in "hl"]
            wsm = {n: [sb(f"w{n}{p}", [128, NK, D], F32R) for p in "hl"] for n in "qkv"}
            stt, mv, sm = sb("stt", [128, NT, 6]), sb("mv", [128, NT, 2]), sb("sm", [128, 4, NT])
            itk = sb("itk", [1, B], I32)
            tsb = sb("tsb", [128, B], I32)
            frq = sb("frq", [128, 1])
            em = sb("em", [128, 8, 2 * B])
            bqk = sb("bqk", [128, 2, NK])
            bvb = sb("bvb", [128, D])
            ss = sb("ss", [128, B, 2 * D])
            x2 = [sb(f"x2{i}", [128, NT, D]) for i in range(2)]
            v17 = sb("v17", [128, NT, H, VW])
            qf, qr = [sb(f"qf{i}", [128, NK, S]) for i in range(2)], sb("qr", [128, NK, S])
            parts = [sb(f"parts{i}", [128, 3, NK, S], BF16) for i in range(2)]

            d_c, d_i = slot("c"), slot("i")
            d_x, d_xt, d_wi, d_wo = [slot(f"x{i}") for i in range(2)], slot("xt"), slot("wi"), slot("wo")
            d_s, d_bi = [slot(f"s{i}") for i in range(2)], [slot(f"bi{i}") for i in range(2)]
            expert = {}

            def load_x(b, *waits):
                return sp.dma(d_x[b % 2], xs[b % 2][:, :, :], rows(x[b]), *waits)

            def load_xt(b, *waits):
                return sp.dma(d_xt, xt[:, :, :], x_t[b].rearrange("(k p) s -> p k s", p=128), *waits)

            def ix(b):
                return bass.ds(expert[b], 1)

            def dyn(sl, dst, src, *waits):
                sl[1] += 16
                sp.items.append((lambda e: e.dma_start(dst(), src()), [w for w in waits if w], (sl[0], 16)))
                return (sl[0], sl[1])

            def load_wi(b, *waits):
                return dyn(d_wi, lambda: wi_f[:, :, :], lambda: Wi[ix(b), :, :].rearrange("e (k p) i -> p (e k) i", p=128), *waits)

            def load_wo(b, *waits):
                return dyn(d_wo, lambda: wo_f[:, :, :], lambda: Wo0[ix(b), :, :].rearrange("e (m p) n -> p (e m) n", p=128), *waits)

            def load_bi(b, *waits):
                return dyn(d_bi[b % 2], lambda: bis[b % 2][:, :], lambda: bi[ix(b), :, :].rearrange("e p m -> (e p) m"), *waits)

            def load_small(b, *waits):
                for n, a in enumerate((bo0, gam, bet)):
                    k = dyn(d_s[b % 2], lambda n=n: ob[b % 2][:, n, :], lambda a=a: a[ix(b), :].broadcast_to([128, D]), *waits)
                return k

            def read_experts(e):
                for b in range(B):
                    expert[b] = e.value_load(itk[0:1, b:b + 1], min_val=0, max_val=7)

            t_itk = sp.dma(d_i, itk[:, :], itok.rearrange("(a b) -> a b", a=1))
            t_xt = {0: load_xt(0)}
            sp.dma(d_c, tsb[:, :], tstep.rearrange("(a b) -> a b", a=1).broadcast_to([128, B]))
            t_e = sp.dma(d_c, frq[:, :], freqs)
            sp.wait(t_itk)
            sp.items.append((read_experts, [], None))
            t_wi, t_bi, t_wo, t_x, t_sm = {0: load_wi(0)}, {0: load_bi(0)}, {0: load_wo(0)}, {0: load_x(0)}, {0: load_small(0)}
            wstage = {"q": y1, "k": r1, "v": xb[1]}
            wad, bad, emo = qf[0], qr[0:B, 0, :], qr[0:B, 1, :]
            d_w = slot("w")
            sp.wait(t_e)
            sp.dma(d_w, wad[:, :, :], Wada.rearrange("(k p) n -> p k n", p=128))
            sp.dma(d_w, bad, bada.rearrange("(a n) -> a n", a=1).broadcast_to([B, 2 * D]))
            for n, a in ((0, bq), (1, bk)):
                sp.dma(d_w, bqk[:, n, :], a)
            sp.dma(d_w, bvb[:, :], bv.rearrange("(a n) -> a n", a=1).broadcast_to([128, D]))
            for n, w in (("q", Wq), ("k", Wk), ("v", Wv)):
                t_c = sp.dma(d_w, wstage[n][:, 0:NK, :], w.rearrange("(k p) n -> p k n", p=128))
            t_x[1], t_sm[1], t_bi[1] = load_x(1), load_small(1), load_bi(1)

            tk, t_w = {}, {}

            e_, n_, r_, w_ = (em[:, i, 0:B] for i in range(4))
            sc_ = [em[:, 4, 0:B], em[:, 4, B:2 * B]]
            k = dve.op(lambda e: e.tensor_copy(w_, tsb[:, :]), t_e)
            k = dve.op(lambda e: e.tensor_scalar(e_, w_, 0.01, None, ALU.mult), k)
            k = dve.op(lambda e: e.tensor_scalar(n_, e_, 4097.0, None, ALU.mult), k)
            k = dve.op(lambda e: e.tensor_tensor(r_, n_, e_, ALU.subtract), k)
            k = dve.op(lambda e: e.tensor_tensor(n_, n_, r_, ALU.subtract), k)
            k = dve.op(lambda e: e.tensor_tensor(r_, e_, n_, ALU.subtract), k)
            k = dve.op(lambda e: e.scalar_tensor_tensor(out=w_, in0=n_, scalar=-100.0, in1=w_, op0=ALU.mult, op1=ALU.add), k)
            k = dve.op(lambda e: e.scalar_tensor_tensor(out=w_, in0=r_, scalar=-100.0, in1=w_, op0=ALU.mult, op1=ALU.add), k)
            k = dve.op(lambda e: e.scalar_tensor_tensor(out=e_, in0=w_, scalar=0.01, in1=e_, op0=ALU.mult, op1=ALU.add), k)
            k = dve.op(lambda e: e.tensor_scalar(e_, e_, 4000.0, None, ALU.mult), k)
            k = dve.op(lambda e: e.tensor_scalar(e_, e_, frq[:, 0:1], None, ALU.mult), k)
            t_sin = []
            PI = 3.1415925
            for c in range(2):
                k = dve.op(lambda e, c=c: e.tensor_scalar(n_, e_, 0.15915494309189535, 0.25 * c, ALU.mult, ALU.add), k)
                k = dve.op(lambda e: e.tensor_scalar(n_, n_, 12582912.0, None, ALU.add), k)
                k = dve.op(lambda e: e.tensor_scalar(n_, n_, -12582912.0, None, ALU.add), k)
                k = dve.op(lambda e: e.scalar_tensor_tensor(out=r_, in0=n_, scalar=-6.28125, in1=e_, op0=ALU.mult, op1=ALU.add), k)
                k = dve.op(lambda e: e.scalar_tensor_tensor(out=r_, in0=n_, scalar=-0.0019350051879882812, in1=r_, op0=ALU.mult, op1=ALU.add), k)
                k = dve.op(lambda e: e.scalar_tensor_tensor(out=r_, in0=n_, scalar=-3.0199159819e-07, in1=r_, op0=ALU.mult, op1=ALU.add), k)
                if c:
                    k = dve.op(lambda e: e.tensor_scalar(r_, r_, 1.5707963267948966, None, ALU.add), k)
                k = dve.op(lambda e, c=c: e.tensor_scalar(sc_[c], r_, PI, -PI, ALU.min, ALU.max), k)
                t_sin.append(k)
            sn, ex = em[:, 5, :], em[:, 6, :]
            ta = act.op(lambda e: e.activation(sn, em[:, 4, :], ACT.Sin), *t_sin)
            ta2 = act.op(lambda e: e.activation(ex, sn, ACT.Exp, scale=-1.0), ta)

            def embed():
                k = dve.op(lambda e: e.tensor_scalar(ex, ex, 1.0, None, ALU.add), ta2)
                k = dve.op(lambda e: e.reciprocal(ex, ex), k)
                t_sil = dve.op(lambda e: e.tensor_tensor(ex, ex, sn, ALU.mult), k)
                t_bad = dve.op(lambda e: e.tensor_scalar(bad[:, 0:D], bad[:, 0:D], 1.0, None, ALU.add), t_c)
                for c in range(2):
                    t = pe.op(lambda e, c=c: e.matmul(psQ[0][0:B, :], em[:, 6, c * B:(c + 1) * B], wad[:, c, :], start=c == 0, stop=c == 1),
                              t_sil, t_c, inc=c == 1)
                k = dve.op(lambda e: e.tensor_tensor(emo, psQ[0][0:B, :], bad, ALU.add), t, t_bad)
                k = sp.dma(d_c, sc_ss[:, :], emo, k)
                tk["emb"] = sp.dma(d_c, ss[:, :, :], sc_ss.unsqueeze(0).broadcast_to([128, B, 2 * D]), k)

            def split_small():
                for n in "qkv":
                    src, hl = wstage[n][:, 0:NK, :], wsm[n]
                    k = act.op(lambda e, hl=hl, src=src: e.activation(hl[0][:, :, :], src, ACT.Copy), t_c)
                    t_w[n] = dve.op(lambda e, hl=hl, src=src: e.tensor_tensor(hl[1][:, :, :], src, hl[0][:, :, :].bitcast(F32), ALU.subtract), k)

            def split(n, b, src, dst, t_src, q, parts, *free):
                w = src.shape[1] // parts
                for i in range(parts):
                    sl = slice(i * w, (i + 1) * w)
                    k = act.op(lambda e, sl=sl: e.activation(dst[0][:, sl, :], src[:, sl, :], ACT.Copy), t_src, *free)
                    lo = dve if parts > 1 and i % 2 == 0 else q
                    k = lo.op(lambda e, sl=sl: e.tensor_tensor(dst[1][:, sl, :], src[:, sl, :], dst[0][:, sl, :].bitcast(F32), ALU.subtract), k, *free)
                    tk.setdefault((n, b), []).append(k)

            def split_wi(b, parts, *free):
                split("wi", b, wi_f, wi_s, t_wi[b], pool, parts, *free)
                if b + 1 < B:
                    t_wi[b + 1] = load_wi(b + 1, *tk["wi", b])

            def split_wo(b, *free):
                split("wo", b, wo_f, wo_s, t_wo[b], pool, 1, *free)
                if b + 1 < B:
                    t_wo[b + 1] = load_wo(b + 1, *tk["wo", b])

            def split_xt(b, q, *free):
                split("xT", b, xt, xT, t_xt[b], q, 1, *free)
                if b + 1 < B:
                    t_xt[b + 1] = load_xt(b + 1, *tk["xT", b])

            def turn(src, dst, t_src, dst_free):
                for kk in range(NK):
                    for t in range(NT):
                        p = pe.op(lambda e, kk=kk, t=t: e.transpose(psX[:, kk, t * 128:(t + 1) * 128], src[:, t, kk * 128:(kk + 1) * 128], idf[:, :]),
                                  t_src, tk.get("psX"), t_idf, inc=(kk == NK - 1 and t == NT - 1))
                k = act.op(lambda e: e.activation(dst[0][:, :, :], psX[:, :, :], ACT.Copy), p, dst_free)
                tk["psX"] = dve.op(lambda e: e.tensor_tensor(dst[1][:, :, :], psX[:, :, :], dst[0][:, :, :].bitcast(F32), ALU.subtract), k)
                return tk["psX"]

            def hidden(b, m):
                ms = slice(m * 128, (m + 1) * 128)
                p = mm3(psH[m % 2][:, :], [([w[:, kk, ms] for w in wi_s], [z[:, kk, :] for z in xT]) for kk in range(NK)],
                        *tk["wi", b], *tk["xT", b], tk.get(("gelu_ps", m % 2)))
                f = hf[m % 3]
                g = act.op(lambda e: e.activation(f[:, :], psH[m % 2][:, :], ACT.Gelu, bias=bis[b % 2][:, m:m + 1]),
                           p, t_bi[b], tk.get(("hf", m % 3)))
                tk["gelu_ps", m % 2] = g
                k = act.op(lambda e: e.activation(hT[0][:, m, :], f[:, :], ACT.Copy), g, tk.get(("O", b - 1)))
                k = dve.op(lambda e: e.tensor_tensor(hT[1][:, m, :], f[:, :], hT[0][:, m, :].bitcast(F32), ALU.subtract), k)
                tk["hf", m % 3] = k
                tk["H", b], tk["hT", b] = p, k
                if m == NM - 1 and b + 2 < B:
                    t_bi[b + 2] = load_bi(b + 2, g)

            def down(b, t):
                ts = slice(t * 128, (t + 1) * 128)
                tk["O", b] = mm3(psO[:, t, :], [([z[:, m, ts] for z in hT], [w[:, m, :] for w in wo_s]) for m in range(NM)],
                                 tk["hT", b], *tk["wo", b], tk.get(("r1", b - 1)))

            def add_bo(b):
                tk["xb", b] = pool.op(lambda e: e.tensor_tensor(xb[b % 2][:, :, :], xs[b % 2][:, :, :], bc(ob[b % 2][:, 0, :], NT), ALU.add),
                                      t_x[b], t_sm[b], tk.get(("r1", b - 2)), t_w["v"] if b else None)
                if b + 2 < B:
                    t_x[b + 2] = load_x(b + 2, tk["xb", b])

            def norms(b):
                o = ob[b % 2]
                k = dve.op(lambda e: e.tensor_tensor(r1[:, :, :], psO[:, :, :], xb[b % 2][:, :, :], ALU.add), tk["xb", b], tk["O", b], t_w["k"])
                tk["r1", b] = k
                yield
                k = yield from layernorm(r1, y1, stt, mv, sm, 1e-12, k, t_w["q"])
                k = dve.op(lambda e: e.tensor_tensor(y1[:, :, :], y1[:, :, :], bc(o[:, 1, :], NT), ALU.mult), k, t_sm[b])
                yield
                k = dve.op(lambda e: e.tensor_tensor(y1[:, :, :], y1[:, :, :], bc(o[:, 2, :], NT), ALU.add), k)
                if b + 2 < B:
                    t_sm[b + 2] = load_small(b + 2, k, tk["xb", b])
                yield
                z = x2[b % 2]
                k = yield from layernorm(y1, z, stt, mv, sm, 1e-5, k, tk.get(("x2T", b - 2)), tk.get(("sx2", b - 2)))
                k = dve.op(lambda e: e.tensor_tensor(z[:, :, :], z[:, :, :], bc(ss[:, b, 0:D], NT), ALU.mult), k, tk["emb"])
                yield
                tk["x2", b] = pool.op(lambda e: e.tensor_tensor(z[:, :, :], z[:, :, :], bc(ss[:, b, D:2 * D], NT), ALU.add), k)
                tk["sx2", b] = sp.dma(d_x2[b % 2], rows(sc_x2[b]), z[:, :, :], tk["x2", b])

            d_p, d_v, d_x2 = [slot(f"p{i}") for i in range(2)], slot("v"), [slot(f"x2{i}") for i in range(2)]

            def qkv(b):
                for n, (w, scale) in enumerate((("q", 0.25), ("k", 1.0))):
                    for mt in range(NK):
                        ms = slice(mt * 128, (mt + 1) * 128)
                        p = mm3(psQ[mt][:, :], [([u[:, kk, ms] for u in wsm[w]], [z[:, kk, :] for z in x2T]) for kk in range(NK)],
                                t_w[w], tk["x2T", b], tk.get(("psQ", mt)), tk["emb"])
                        k = act.op(lambda e, mt=mt, n=n, scale=scale: e.activation(qf[n][:, mt, :], psQ[mt][:, :], ACT.Identity,
                                                                                   bias=bqk[:, n, mt:mt + 1], scale=scale),
                                   p, t_bq, tk.get(("qf", n)), tk["emb"])
                        tk["psQ", mt] = k
                        yield
                    pt, free = parts[n], tk.get(("parts", n))
                    k = act.op(lambda e, pt=pt, n=n: e.activation(pt[:, 0, :, :], qf[n][:, :, :], ACT.Copy), k, free)
                    k = dve.op(lambda e, pt=pt, n=n: e.tensor_tensor(qr[:, :, :], qf[n][:, :, :], pt[:, 0, :, :], ALU.subtract), k, tk.get("qr"), tk["emb"])
                    tk["qf", n] = k
                    k = act.op(lambda e, pt=pt: e.activation(pt[:, 1, :, :], qr[:, :, :], ACT.Copy), k)
                    k = pool.op(lambda e, pt=pt: e.tensor_tensor(pt[:, 2, :, :], qr[:, :, :], pt[:, 1, :, :], ALU.subtract), k)
                    tk["qr"] = k
                    for c in range(3):
                        tk["parts", n] = sp.dma(d_p[n], sc_qk[b, n, c].rearrange("(k p) s -> p k s", p=128), pt[:, c, :, :], k)
                for half in range(2):
                    for t in (2 * half, 2 * half + 1):
                        ts = slice(t * 128, (t + 1) * 128)
                        p = mm3(psQ[half][:, (t % 2) * D:(t % 2 + 1) * D],
                                [([z[:, kk, ts] for z in x2T], [u[:, kk, :] for u in wsm["v"]]) for kk in range(NK)],
                                t_w["v"], tk.get(("psQ", half)))
                    for t in (2 * half, 2 * half + 1):
                        k = dve.op(lambda e, t=t, half=half: e.tensor_tensor(
                            v17[:, t, :, 0:HD], psQ[half][:, (t % 2) * D:(t % 2 + 1) * D].rearrange("p (h d) -> p h d", d=HD),
                            bvb[:, :].rearrange("p (h d) -> p h d", d=HD), ALU.add), p, tk.get("sv"), t_c)
                    tk["psQ", half] = k
                    yield
                tk["V", b] = p
                tk["sv"] = sp.dma(d_v, rows(sc_v[b]), v17[:, :, :, :].rearrange("p t h v -> p t (h v)"), k, t_one)
                t_b[b] = [tk["parts", 0], tk["parts", 1], tk["sv"]]

            split_xt(0, dve)
            split_wi(0, 2)
            t_bq = dve.op(lambda e: e.tensor_scalar(bqk[:, 0, :], bqk[:, 0, :], 0.25, None, ALU.mult), t_c)
            t_one = dve.op(lambda e: e.memset(v17[:, :, :, HD:VW], 1.0))
            add_bo(0)
            split_wo(0)
            side = iter(())
            for i in range(B + 2):
                if 1 <= i <= B:
                    side = norms(i - 1)
                    advance(side, 1)
                if 1 <= i < B:
                    add_bo(i)
                for m in range(NM):
                    if i < B:
                        hidden(i, m)
                    if m == 3 and i >= 2:
                        tk["x2T", i - 2] = turn(x2[i % 2], x2T, tk["x2", i - 2], tk.get(("V", i - 3)))
                    if m == 3 and i == 0:
                        embed()
                    if m == 5 and i == 0:
                        split_small()
                if i + 1 < B:
                    split_xt(i + 1, pool, tk["H", i])
                q = qkv(i - 2) if i >= 2 else iter(())
                for n in range(6):
                    advance(q, 1)
                    advance(side, 3)
                    if n == 1 and i + 1 < B:
                        split_wi(i + 1, 1, tk["H", i])
                advance(q, 1)
                if i < B:
                    for t in range(NT):
                        down(i, t)
                        advance(side, 3)
                    if i + 1 < B:
                        split_wo(i + 1, tk["O", i])
                advance(side, 1000)
        barrier()

        @phase
        def _(st):
            def sb(name, shape, dt=F32):
                return sbuf(st, name, shape, dt)

            NB, NP, NS, NTB = 6, 6, 3, 3
            psS = [st.enter_context(nc.psum_tensor(f"psS{i}", [128, 512], F32)) for i in range(NS)]
            psT = [st.enter_context(nc.psum_tensor(f"psT{i}", [128, NT, 128], F32)) for i in range(NTB)]
            psV = st.enter_context(nc.psum_tensor("psV", [128, 512], F32))
            psC = st.enter_context(nc.psum_tensor("psC", [128, NT, 4, 32], F32))

            bt = [sb(f"bt{i}", [128, NT, S]) for i in range(NB)]
            pt = [sb(f"pt{i}", [128, NT, S]) for i in range(NP)]
            qs = [sb(f"qs{i}", [KR, 8, S], BF16) for i in range(2)]
            ks = [sb(f"ks{i}", [KR, 8, S], BF16) for i in range(2)]
            vs = [sb(f"vs{i}", [128, NT, H, VW]) for i in range(2)]
            mk = [sb(f"mk{i}", [128, NT, S], U8) for i in range(2)]
            mb = [sb(f"mb{i}", [128, NT, S], BF16) for i in range(2)]
            na = [sb(f"na{i}", [128, NT]) for i in range(2)]
            nm = sb("nm", [128, 16])
            cv = sb("cv", [128, 512])
            den = sb("den", [128, NT, 4])
            cx = [sb(f"cx{i}", [128, NT, D]) for i in range(2)]
            d_b = [slot(f"b{i}") for i in range(NB)]
            d_q = [slot(f"q{i}") for i in range(2)]
            d_m = [slot(f"m{i}") for i in range(2)]
            d_o = [slot(f"o{i}") for i in range(2)]
            N = B * H * NT
            tk = {}
            t_vz = dve.op(lambda e: e.memset(psV[:, :], 0.0))

            def load_qk(n):
                b, half = divmod(n, 2)
                free = tk.get(("QK", 32 * (n - 1) - 1))
                for dst, w in ((qs, 0), (ks, 1)):
                    for i, c in enumerate(TERMS):
                        src = sc_qk[b, w, c[w]].rearrange("(h d) s -> d h s", d=HD)[:, 8 * half:8 * half + 8, :]
                        tk["qs", n] = sp.dma(d_q[n % 2], dst[n % 2][i * HD:(i + 1) * HD, :, :], src, free)

            def load_batch(b):
                free = [tk.get(("PV", 4 * (b - 1) - 1)), tk.get(("mb", b - 2)), tk.get(("na", b - 2))]
                sp.dma(d_m[b % 2], vs[b % 2][:, :, :, :].rearrange("p t h v -> p t (h v)"), rows(sc_v[b]), *free)
                tk["vm", b] = sp.dma(d_m[b % 2], mk[b % 2][:, :, :], rows(mask[b]), *free)

            def read_mask(b, t):
                tk["mb", b] = dve.op(lambda e: e.tensor_scalar(mb[b % 2][:, t, :], mk[b % 2][:, t, :], NEG, None, ALU.mult),
                                     tk["vm", b], tk.get(("QK", 64 * (b - 1) - 1)), tk.get(("M", 16 * (b - 1) - 1)), tk.get(("M", 16 * (b - 1) - 2)))
                k = dve.op(lambda e: e.tensor_reduce(na[b % 2][:, t:t + 1], mk[b % 2][:, t, :], AX.X, ALU.min), tk["vm", b], tk.get(("C", 4 * (b - 1) - 1)))
                tk["na", b] = dve.op(lambda e: e.tensor_scalar(na[b % 2][:, t:t + 1], na[b % 2][:, t:t + 1], -1.0, 1.0, ALU.mult, ALU.add), k)

            def load_bias(u):
                tk["bt", u] = sp.dma(d_b[u % NB], bt[u % NB][:, :, :], rows(bias[u // H, u % H]), tk.get(("T", 4 * (u - NB) + 3)))

            def on_pool(u):
                return u % 4 != 3

            def add_mask(u):
                t, m = bt[u % NB], mb[u // H % 2]
                tk["M", u] = pool.op(lambda e: e.tensor_tensor(t[:, :, :], t[:, :, :], m[:, :, :], ALU.add), tk["bt", u], tk["mb", u // H])

            def scores(n):
                u, t = divmod(n, NT)
                b, h = divmod(u, H)
                g = u // 8 % 2
                ts = slice(t * 128, (t + 1) * 128)
                if not on_pool(u):
                    pe.op(lambda e: e.matmul(psS[n % NS][:, :], idb[:, :], mb[b % 2][:, t, :], start=True, stop=False),
                          tk["mb", b], tk.get(("max", n - NS)), t_idb, inc=False)
                tk["QK", n] = pe.op(lambda e: e.matmul(psS[n % NS][:, :], qs[g][:, h % 8, ts], ks[g][:, h % 8, :], start=on_pool(u), stop=True),
                                    tk["qs", u // 8], tk.get(("max", n - NS)))
                s = bt[u % NB][:, t, :]
                tk["max", n] = dve.op(lambda e: e.tensor_tensor_reduce(s, psS[n % NS][:, :], s, -1.0, 3.0e38, ALU.add, ALU.min,
                                                                       nm[:, n % 16:n % 16 + 1]),
                                      tk["QK", n], tk["bt", u], tk.get(("M", u)), tk.get(("exp", n - 16)))

            def exps(n):
                s = bt[n // NT % NB][:, n % NT, :]
                tk["exp", n] = act.op(lambda e: e.activation(s, s, ACT.Exp, bias=nm[:, n % 16:n % 16 + 1], scale=-1.0), tk["max", n])

            def turn_p(n):
                u, t = divmod(n, NT)
                for kk in range(NT):
                    tk["T", n] = pe.op(lambda e, kk=kk: e.transpose(psT[n % NTB][:, kk, :], bt[u % NB][:, t, kk * 128:(kk + 1) * 128], idf[:, :]),
                                       tk["exp", n], tk.get(("E", n - NTB)), inc=kk == NT - 1)

            def evac(n):
                u, t = divmod(n, NT)
                dst, src = pt[u % NP][:, :, t * 128:(t + 1) * 128], psT[n % NTB][:, :, :]
                if n % 5 in ON_ACT:
                    q, f = act, lambda e: e.activation(dst, src, ACT.Copy)
                else:
                    q, f = dve, lambda e: e.tensor_copy(dst, src)
                tk["E", n] = q.op(f, tk["T", n], tk.get(("PV", u // 4 - 1 if u % 4 >= NP - 4 else u // 4 - 2)) if u >= NP else None)
                tk["Es", u] = tk.get(("Es", u), []) + [tk["E", n]]

            def context(gi, kk):
                b, hg = divmod(gi, 4)
                for g in range(4):
                    u = 4 * gi + g
                    p = pe.op(lambda e, g=g, u=u: e.matmul(
                        psV[32 * g:32 * g + VW, :], vs[b % 2][:, kk, u % H, :], pt[u % NP][:, kk, :], start=kk == 0, stop=kk == NT - 1),
                        *tk["Es", u], tk["vm", b], tk.get(("cv", gi - 1)), t_vz, inc=(kk == NT - 1 and g == 3))
                if kk == NT - 1:
                    tk["PV", gi] = p
                    tk["cv", gi] = act.op(lambda e: e.activation(cv[:, :], psV[:, :], ACT.Copy), p, tk.get(("CT", gi - 1)))

            def finish(gi):
                b, hg = divmod(gi, 4)
                for t in range(NT):
                    p = pe.op(lambda e, t=t: e.transpose(psC[:, t, :, :].rearrange("p a c -> p (a c)"), cv[:, t * 128:(t + 1) * 128], idf[:, :]),
                              tk["cv", gi], tk.get(("C", gi - 1)), inc=t == NT - 1)
                tk["CT", gi] = p
                nb = na[b % 2][:, :].unsqueeze(2).broadcast_to([128, NT, 4])
                k = dve.op(lambda e: e.tensor_tensor(den[:, :, :], psC[:, :, :, HD], nb, ALU.mult), p, tk["na", b], tk.get(("C", gi - 1)))
                k = dve.op(lambda e: e.reciprocal(den[:, :, :], den[:, :, :]), k)
                k = dve.op(lambda e: e.tensor_tensor(den[:, :, :], den[:, :, :], nb, ALU.mult), k)
                dst = cx[b % 2][:, :, 64 * hg:64 * hg + 64].rearrange("p t (g d) -> p t g d", d=HD)
                tk["C", gi] = dve.op(lambda e: e.tensor_tensor(dst, psC[:, :, :, 0:HD], den[:, :, :].unsqueeze(3).broadcast_to([128, NT, 4, HD]), ALU.mult),
                                     k, tk.get(("so", b - 2)))
                if hg == 3:
                    tk["so", b] = sp.dma(d_o[b % 2], rows(sc_c[b]), cx[b % 2][:, :, :], tk["C", gi])

            load_qk(0)
            load_batch(0)
            for t in range(NT):
                read_mask(0, t)
            LAG, ELAG, XLAG, PSTEP, ON_ACT = 4, 0, 1, 2, (0, 2, 4)
            nextb = nextm = 0
            for n in range(N + 40):
                while nextb < min(B * H, n // NT + NB) and (nextb < NB or ("T", 4 * (nextb - NB) + 3) in tk):
                    load_bias(nextb)
                    nextb += 1
                while nextm < min(B * H, n // NT + 3, nextb) and ("mb", nextm // H) in tk:
                    if on_pool(nextm):
                        add_mask(nextm)
                    nextm += 1
                if n < N and n % 32 == 4 and n // 32 + 1 < 2 * B:
                    load_qk(n // 32 + 1)
                if n < N and n % 64 == 28 and n // 64 + 1 < B:
                    load_batch(n // 64 + 1)
                if n < N and n // 64 + 1 < B and n % 64 in (46, 48, 50, 52):
                    read_mask(n // 64 + 1, n % 64 // 2 - 23)
                if n < N:
                    scores(n)
                m = n - LAG
                if 0 <= m < N:
                    turn_p(m)
                m = n - LAG - ELAG
                if 0 <= m < N:
                    evac(m)
                m = n - XLAG
                if 0 <= m < N:
                    exps(m)
                for kk in range(NT):
                    m = n - LAG - ELAG - 1 - PSTEP * kk
                    if 0 <= m < N and m % 16 == 15:
                        context(m // 16, kk)
                m = n - LAG - ELAG - 3 - 3 * PSTEP
                if 0 <= m < N and m % 16 == 15:
                    finish(m // 16)
        barrier()

        @phase
        def _(st):
            def sb(name, shape, dt=F32):
                return sbuf(st, name, shape, dt)

            psX = st.enter_context(nc.psum_tensor("psX2", [128, NK, 512], F32))
            psH = [st.enter_context(nc.psum_tensor(f"psH2{i}", [128, 512], F32)) for i in range(2)]
            psO = st.enter_context(nc.psum_tensor("psO2", [128, NT, D], F32))
            psA = st.enter_context(nc.psum_tensor("psA2", [128, NT, D], F32))
            cs = [sb(f"cc{i}", [128, NT, D]) for i in range(2)]
            xs = [sb(f"cx2{i}", [128, NT, D]) for i in range(2)]
            x3 = [sb(f"x3{i}", [128, NT, D]) for i in range(2)]
            hl = [sb(f"hl{i}", [128, NT, D]) for i in range(2)]
            os_ = [sb(f"os{i}", [128, NT, D]) for i in range(2)]
            cT = [sb(f"cT{n}", [128, NK, S], F32R) for n in "hl"]
            lT = [sb(f"lT{n}", [128, NK, S], F32R) for n in "hl"]
            hf = [sb(f"chf{i}", [128, S]) for i in range(3)]
            hT = [sb(f"chT{n}", [128, NM, S], F32R) for n in "hl"]
            ws = {"o": (Wo, NK, D), "1": (W1, NK, I), "2": (W2, NM, D)}
            wf = {n: sb(f"cwf{n}", [128, k, w]) for n, (_, k, w) in ws.items()}
            wl = {n: [sb(f"cw{n}{p}", [128, k, w], F32R) for p in "hl"] for n, (_, k, w) in ws.items()}
            b1c = sb("b1c", [128, NM])
            rb = sb("rb", [128, 4, D])
            stt, mv, sm = sb("cstt", [128, NT, 6]), sb("cmv", [128, NT, 2]), sb("csm", [128, 4, NT])
            d_c = slot("cc")
            for n, (w, k, wd) in ws.items():
                sp.dma(d_c, wf[n][:, :, :], w.rearrange("(k p) n -> p k n", p=128))
            sp.dma(d_c, b1c[:, :], b1)
            for n, a in enumerate((bo, g2, be2, b2)):
                t_c = sp.dma(d_c, rb[:, n, :], a.rearrange("(a n) -> a n", a=1).broadcast_to([128, D]))
            d_l, d_out = [slot(f"cl{i}") for i in range(2)], [slot(f"out{i}") for i in range(2)]
            tk, t_w = {}, {}

            def load(b, *waits):
                sp.dma(d_l[b % 2], cs[b % 2][:, :, :], rows(sc_c[b]), *waits)
                tk["ld", b] = sp.dma(d_l[b % 2], xs[b % 2][:, :, :], rows(sc_x2[b]), *waits)

            load(0)
            load(1)
            for n in ws:
                k = act.op(lambda e, n=n: e.activation(wl[n][0][:, :, :], wf[n][:, :, :], ACT.Copy), t_c)
                t_w[n] = dve.op(lambda e, n=n: e.tensor_tensor(wl[n][1][:, :, :], wf[n][:, :, :], wl[n][0][:, :, :].bitcast(F32), ALU.subtract), k)

            def turn(src, dst, t_src, dst_free):
                for kk in range(NK):
                    for t in range(NT):
                        p = pe.op(lambda e, kk=kk, t=t: e.transpose(psX[:, kk, t * 128:(t + 1) * 128], src[:, t, kk * 128:(kk + 1) * 128], idf[:, :]),
                                  t_src, tk.get("psX"), inc=(kk == NK - 1 and t == NT - 1))
                k = act.op(lambda e: e.activation(dst[0][:, :, :], psX[:, :, :], ACT.Copy), p, dst_free)
                k = dve.op(lambda e: e.tensor_tensor(dst[1][:, :, :], psX[:, :, :], dst[0][:, :, :].bitcast(F32), ALU.subtract), k)
                tk["psX"] = k
                return k

            def norms(b):
                k = dve.op(lambda e: e.tensor_tensor(x3[b % 2][:, :, :], psA[:, :, :], xs[b % 2][:, :, :], ALU.add),
                           tk["xb", b], tk["A", b], tk.get(("out", b - 2)))
                tk["x3", b] = k
                yield
                h = hl[b % 2]
                k = yield from layernorm(x3[b % 2], h, stt, mv, sm, 1e-5, k, tk.get(("lT", b - 2)))
                tk["ln", b] = k
                k = dve.op(lambda e: e.tensor_tensor(h[:, :, :], h[:, :, :], bc(rb[:, 1, :], NT), ALU.mult), k)
                yield
                tk["h", b] = pool.op(lambda e: e.tensor_tensor(h[:, :, :], h[:, :, :], bc(rb[:, 2, :], NT), ALU.add), k)
                tk["x3b", b] = pool.op(lambda e: e.tensor_tensor(x3[b % 2][:, :, :], x3[b % 2][:, :, :], bc(rb[:, 3, :], NT), ALU.add), tk["ln", b])
                if b + 2 < B:
                    load(b + 2, tk["cT", b], tk["x3", b])

            def turn_c(b):
                tk["cT", b] = turn(cs[b % 2], cT, tk["ld", b], tk.get(("A", b - 1)))
                tk["xb", b] = pool.op(lambda e: e.tensor_tensor(xs[b % 2][:, :, :], xs[b % 2][:, :, :], bc(rb[:, 0, :], NT), ALU.add), tk["ld", b], t_c)

            def project(b):
                for t in range(NT):
                    ts = slice(t * 128, (t + 1) * 128)
                    p = mm3(psA[:, t, :], [([z[:, kk, ts] for z in cT], [u[:, kk, :] for u in wl["o"]]) for kk in range(NK)],
                            tk["cT", b], t_w["o"], tk.get(("x3", b - 1)))
                tk["A", b] = p

            def turn_l(b):
                tk["lT", b] = turn(hl[b % 2], lT, tk["h", b], tk.get(("H", b - 1)))

            def up(b, m):
                ms = slice(m * 128, (m + 1) * 128)
                p = mm3(psH[m % 2][:, :], [([w[:, kk, ms] for w in wl["1"]], [z[:, kk, :] for z in lT]) for kk in range(NK)],
                        t_w["1"], tk["lT", b], tk.get(("g", m % 2)))
                f = hf[m % 3]
                g = act.op(lambda e: e.activation(f[:, :], psH[m % 2][:, :], ACT.Gelu_apprx_sigmoid, bias=b1c[:, m:m + 1]),
                           p, t_c, tk.get(("hf", m % 3)))
                tk["g", m % 2] = g
                k = act.op(lambda e: e.activation(hT[0][:, m, :], f[:, :], ACT.Copy), g, tk.get(("O", b - 1)))
                k = dve.op(lambda e: e.tensor_tensor(hT[1][:, m, :], f[:, :], hT[0][:, m, :].bitcast(F32), ALU.subtract), k)
                tk["hf", m % 3] = k
                tk["H", b] = p
                tk["hT", b] = k

            def down(b, t):
                ts = slice(t * 128, (t + 1) * 128)
                tk["O", b] = mm3(psO[:, t, :], [([z[:, m, ts] for z in hT], [w[:, m, :] for w in wl["2"]]) for m in range(NM)],
                                 tk["hT", b], t_w["2"], tk.get(("out", b - 1)))

            def store(b):
                k = dve.op(lambda e: e.tensor_tensor(os_[b % 2][:, :, :], psO[:, :, :], x3[b % 2][:, :, :], ALU.add),
                           tk["O", b], tk["x3b", b], tk.get(("so", b - 2)))
                tk["out", b] = k
                tk["so", b] = sp.dma(d_out[b % 2], rows(out[b]), os_[b % 2][:, :, :], k)

            turn_c(0)
            project(0)
            advance(norms(0), 1000)
            turn_l(0)
            for b in range(B):
                more = b + 1 < B
                if more:
                    turn_c(b + 1)
                side = iter(())
                for m in range(NM):
                    up(b, m)
                    if more and m == 2:
                        project(b + 1)
                        side = norms(b + 1)
                    advance(side, 3)
                advance(side, 1000)
                for t in range(NT - 1):
                    down(b, t)
                if more:
                    turn_l(b + 1)
                down(b, NT - 1)
                store(b)
        sp.wait(*[(s[0], s[1]) for s in slots if s[1]])

        block = ctx.enter_context(nc.Block())

        @block.sync
        def _(e):
            sp.emit(e)

        @block.tensor
        def _(e):
            pe.emit(e)

        @block.scalar
        def _(e):
            act.emit(e)

        @block.vector
        def _(e):
            dve.emit(e)

        @block.gpsimd
        def _(e):
            pool.emit(e)


_INS = ["x", "itok_B_0_7", "itok_B_34_63", "fside_Bx16xSxS_0", "mask_Bx1xSxS_bk0",
        "L0_cond_Wi", "L0_cond_bi", "L0_cond_Wo", "L0_cond_bo", "L0_cond_gamma", "L0_cond_beta",
        "L1_cond_W_ada", "L1_cond_b_ada", "L1_cond_Wq", "L1_cond_bq", "L1_cond_Wk", "L1_cond_bk",
        "L1_cond_Wv", "L1_cond_bv", "L1_cond_Wo", "L1_cond_bo", "L1_cond_W1", "L1_cond_b1",
        "L1_cond_W2", "L1_cond_b2", "L1_cond_g2", "L1_cond_beta2"]
_COLS = ["L0_cond_bi", "L1_cond_bq", "L1_cond_bk", "L1_cond_b1"]


def kernel(**inputs):
    import numpy as np
    import concourse.bacc as bacc
    from concourse.bass_utils import run_bass_kernel_spmd as run

    nc = bacc.Bacc("TRN2", target_bir_lowering=False, num_devices=1)
    arrays, args = {}, []

    def give(name, a):
        arrays[name] = a
        args.append(nc.dram_tensor(name, a.shape, mybir.dt.from_np(a.dtype), kind="ExternalInput").ap())

    for name in _INS:
        a = np.ascontiguousarray(inputs[name])
        if name.startswith("mask"):
            a = a.reshape(B, S, S)
        if name in _COLS:
            a = np.ascontiguousarray(np.swapaxes(a.reshape(a.shape[:-1] + (-1, 128)), -1, -2))
        give(f"in_{name}", a)
    a = np.ascontiguousarray(np.swapaxes(np.asarray(inputs["x"]), 1, 2))
    arrays["in_x_t"] = a
    args.insert(1, nc.dram_tensor("in_x_t", a.shape, F32, kind="ExternalInput").ap())
    give("ident", np.eye(128, dtype=np.float32))
    step = np.float32(-np.log(10000.0) / 127)
    give("freqs", np.exp(np.arange(128, dtype=np.float32) * step).astype(np.float32).reshape(128, 1))
    args.append(nc.dram_tensor("out_0", (B, S, D), F32, kind="ExternalOutput").ap())
    program(nc, *args)
    r = run(nc, [arrays], core_ids=[0])
    return r.results[0]["out_0"]
```

```python
from contextlib import ExitStack

import concourse.bass as bass
from concourse import mybir

F32 = mybir.dt.float32
F32R = mybir.dt.float32r
BF16 = mybir.dt.bfloat16
I32 = mybir.dt.int32
U8 = mybir.dt.uint8
ALU = mybir.AluOpType
ACT = mybir.ActivationFunctionType
AX = mybir.AxisListType

B, S, D, I, H, HD = 8, 512, 256, 1024, 16, 16
NT = S // 128
NK = D // 128
NM = I // 128
VW = HD + 1
NEG = -1.0e30
TERMS = [(0, 0), (0, 1), (1, 0), (1, 1), (0, 2), (2, 0)]
KR = HD * len(TERMS)


class Queue:

    def __init__(self, nc, ctx, name):
        self.nc, self.ctx, self.name = nc, ctx, name
        self.items = []
        self.phase()

    def phase(self):
        self.n = 0
        self.sem = self.ctx.enter_context(self.nc.semaphore(f"s_{self.name}{len(self.items)}"))

    def op(self, fn, *waits, inc=True):
        if inc:
            self.n += 1
        self.items.append((fn, [w for w in waits if w], (self.sem, 1) if inc else None))
        return (self.sem, self.n) if inc else None

    def dma(self, slot, out, in_, *waits, **kw):
        slot[1] += 16
        self.items.append((lambda e: e.dma_start(out, in_, **kw), [w for w in waits if w], (slot[0], 16)))
        return (slot[0], slot[1])

    def wait(self, *waits):
        self.items.append((None, [w for w in waits if w], None))

    def last(self):
        return (self.sem, self.n) if self.n else None

    def emit(self, eng):
        passed = {}
        for fn, waits, inc in self.items:
            for sem, v in waits:
                if passed.get(sem.name, 0) < v:
                    eng.wait_ge(sem, v)
                    passed[sem.name] = v
            if fn is None:
                continue
            ins = fn(eng)
            if inc:
                ins.then_inc(*inc)


def program(nc, x, x_t, itok, tstep, bias, mask, Wi, bi, Wo0, bo0, gam, bet, Wada, bada, Wq, bq, Wk, bk, Wv, bv,
            Wo, bo, W1, b1, W2, b2, g2, be2, ident, freqs, out):
    with ExitStack() as ctx:
        sp, pe, act, dve, pool = (Queue(nc, ctx, n) for n in ("sp", "pe", "act", "dve", "pool"))
        slots = []

        def slot(name):
            s = [ctx.enter_context(nc.semaphore(f"d_{name}")), 0]
            slots.append(s)
            return s

        def dram(name, shape, dt):
            return nc.dram_tensor(name, shape, dt, kind="Internal").ap()

        sc_qk = dram("sc_qk", [B, 2, 3, D, S], BF16)
        sc_v = dram("sc_v", [B, S, H * VW], F32)
        sc_x2 = dram("sc_x2", [B, S, D], F32)
        sc_ss = dram("sc_ss", [B, 2 * D], F32)
        sc_c = dram("sc_c", [B, S, D], F32)

        def rows(a):
            return a.rearrange("(t p) d -> p t d", p=128)

        base = ctx.enter_context(ExitStack())

        def sbuf(stack, name, shape, dt=F32):
            return stack.enter_context(nc.sbuf_tensor(f"t_{name}", shape, dt))

        idf = sbuf(base, "idf", [128, 128])
        idb = sbuf(base, "idb", [128, 128], BF16)
        d_id = slot("id")
        t_idf = sp.dma(d_id, idf[:, :], ident)
        t_idb = dve.op(lambda e: e.tensor_copy(idb[:, :], idf[:, :]), t_idf)

        def turn_over():
            ends = [q.last() for q in (pe, act, dve, pool)] + [(s[0], s[1]) for s in slots if s[1]]
            for q in (pe, act, dve, pool):
                q.phase()
            return ends

        def mm3(dst, pairs, *waits, each=()):
            todo = [(lh[a], rh[c], i, (a, c) == (0, 0)) for i, (lh, rh) in enumerate(pairs) for a, c in ((0, 0), (0, 1), (1, 0))]
            for n, (l, r, i, first) in enumerate(todo):
                end = n == len(todo) - 1
                t = pe.op(lambda e, l=l, r=r, n=n, end=end: e.matmul(dst, l, r, start=n == 0, stop=end),
                          *(waits if n == 0 else ()), *(each[i:i + 1] if first else ()), inc=end)
            return t

        def layernorm(src, dst, st, mv, sm, eps, scale, shift, t_src, *waits):
            ks = []
            for t in range(NT):
                ks.append(dve.op(lambda e, t=t: e.bn_stats(st[:, t, :], src[:, t, :]), t_src))
                yield
            ks = [dve.op(lambda e, t=t: e.bn_aggr(mv[:, t, :], st[:, t, :]), ks[t]) for t in range(NT)]
            yield

            def centre(t):
                return dve.op(lambda e: e.scalar_tensor_tensor(out=dst[:, t, :], in0=src[:, t, :], scalar=mv[:, t, 0:1], in1=scale,
                                                               op0=ALU.subtract, op1=ALU.mult), ks[t], *waits)

            v, y, a, hv = (sm[:, i, :] for i in range(4))
            k = dve.op(lambda e: e.tensor_scalar(v, mv[:, :, 1], eps, None, ALU.add), ks[-1])
            cs = [centre(0)]
            h = dve.op(lambda e: e.tensor_scalar(hv, v, -0.5, None, ALU.mult), k)
            k = dve.op(lambda e: e.tensor_scalar(a.bitcast(I32), v.bitcast(I32), 1, None, ALU.arith_shift_right), k)
            cs.append(centre(1))
            k = dve.op(lambda e: e.tensor_scalar(y.bitcast(I32), a.bitcast(I32), -1.0, 1597463007.0, ALU.mult, ALU.add), k)
            for n in range(3):
                k = dve.op(lambda e: e.tensor_tensor(a, y, y, ALU.mult), k)
                if n < 2:
                    cs.append(centre(2 + n))
                k = dve.op(lambda e: e.tensor_tensor(a, a, hv, ALU.mult), k, h)
                k = dve.op(lambda e: e.scalar_tensor_tensor(out=y, in0=a, scalar=1.5, in1=y, op0=ALU.add, op1=ALU.mult), k)
                yield
            for t in range(NT):
                k2 = dve.op(lambda e, t=t: e.scalar_tensor_tensor(out=dst[:, t, :], in0=dst[:, t, :], scalar=sm[:, 1, t:t + 1], in1=shift,
                                                                  op0=ALU.mult, op1=ALU.add), k, cs[t])
                yield
            return k2

        def advance(steps, n):
            for _ in range(n):
                if next(steps, self_end) is self_end:
                    return

        self_end = object()

        def bc(a, n):
            return a.unsqueeze(1).broadcast_to([128, n, D])

        left = {"stores": []}

        def phase_a(st):
            def sb(name, shape, dt=F32):
                return sbuf(st, name, shape, dt)

            psX = st.enter_context(nc.psum_tensor("psX", [128, NK, 512], F32))
            psH = [st.enter_context(nc.psum_tensor(f"psH{i}", [128, 512], F32)) for i in range(2)]
            psO = st.enter_context(nc.psum_tensor("psO", [128, NT, D], F32))
            psQ = [st.enter_context(nc.psum_tensor(f"psQ{i}", [128, 512], F32)) for i in range(2)]

            wi_f, wo_f = sb("wi_f", [128, NK, I]), sb("wo_f", [128, NM, D])
            wi_s = [sb(f"wi{n}", [128, NK, I], F32R) for n in "hl"]
            wo_s = [sb(f"wo{n}", [128, NM, D], F32R) for n in "hl"]
            hT = [sb(f"hT{n}", [128, NM, S], F32R) for n in "hl"]
            xt = sb("xt", [128, NK, S])
            xT = [sb(f"xT{n}", [128, NK, S], F32R) for n in "hl"]
            hf = [sb(f"hf{i}", [128, S]) for i in range(3)]
            xs = [sb(f"x{i}", [128, NT, D]) for i in range(2)]
            itk = sb("itk", [1, B], I32)
            tsb = sb("tsb", [128, B], I32)
            frq = sb("frq", [128, 1])
            em = sb("em", [128, 8, 2 * B])
            bis = [sb(f"bi{i}", [128, NM]) for i in range(2)]
            ob = [sb(f"ob{i}", [128, 3, D]) for i in range(2)]
            xb = [sb(f"xb{i}", [128, NT, D]) for i in range(2)]
            r1, y1 = (sb(n, [128, NT, D]) for n in ("r1", "y1"))
            x2T = [sb(f"x2T{n}", [128, NK, S], F32R) for n in "hl"]
            wsm = {n: [sb(f"w{n}{p}", [128, NK, D], F32R) for p in "hl"] for n in "qkv"}
            stt, mv, sm = sb("stt", [128, NT, 6]), sb("mv", [128, NT, 2]), sb("sm", [128, 4, NT])
            bqk = sb("bqk", [128, 2, NK])
            bvb = sb("bvb", [128, D])
            ss = sb("ss", [128, B, 2 * D])
            x2 = [sb(f"x2{i}", [128, NT, D]) for i in range(2)]
            v17 = sb("v17", [128, NT, H, VW])
            qf, qr = ([sb(f"{n}{i}", [128, NK, S]) for i in range(2)] for n in ("qf", "qr"))
            parts = [sb(f"parts{i}", [128, 3, NK, S], BF16) for i in range(2)]

            d_c, d_i = slot("c"), slot("i")
            d_x, d_xt, d_wi, d_wo = [slot(f"x{i}") for i in range(2)], slot("xt"), slot("wi"), slot("wo")
            d_s, d_bi = [slot(f"s{i}") for i in range(2)], [slot(f"bi{i}") for i in range(2)]
            expert = {}

            def load_x(b, *waits):
                return sp.dma(d_x[b % 2], xs[b % 2][:, :, :], rows(x[b]), *waits)

            def load_xt(b, *waits):
                return sp.dma(d_xt, xt[:, :, :], x_t[b].rearrange("(k p) s -> p k s", p=128), *waits)

            def ix(b):
                return bass.ds(expert[b], 1)

            def dyn(sl, dst, src, *waits):
                sl[1] += 16
                sp.items.append((lambda e: e.dma_start(dst(), src()), [w for w in waits if w], (sl[0], 16)))
                return (sl[0], sl[1])

            def load_wi(b, *waits):
                return dyn(d_wi, lambda: wi_f[:, :, :], lambda: Wi[ix(b), :, :].rearrange("e (k p) i -> p (e k) i", p=128), *waits)

            def load_wi_part(i):
                sl = slice(i * I // 4, (i + 1) * I // 4)
                return dyn(slot(f"wi{i}"), lambda: wi_f[:, :, sl], lambda: Wi[ix(0), :, sl].rearrange("e (k p) i -> p (e k) i", p=128))

            def load_wo(b, *waits):
                return dyn(d_wo, lambda: wo_f[:, :, :], lambda: Wo0[ix(b), :, :].rearrange("e (m p) n -> p (e m) n", p=128), *waits)

            def load_bi(b, *waits):
                return dyn(d_bi[b % 2], lambda: bis[b % 2][:, :], lambda: bi[ix(b), :, :].rearrange("e p m -> (e p) m"), *waits)

            def load_small(b, *waits):
                for n, a in enumerate((bo0, gam, bet)):
                    k = dyn(d_s[b % 2], lambda n=n: ob[b % 2][:, n, :], lambda a=a: a[ix(b), :].broadcast_to([128, D]), *waits)
                return k

            def read_experts(first, last):
                def read(e):
                    for b in range(first, last):
                        expert[b] = e.value_load(itk[0:1, b:b + 1], min_val=0, max_val=7)
                sp.items.append((read, [], None))

            t_itk = sp.dma(d_i, itk[:, :], itok.rearrange("(a b) -> a b", a=1))
            t_xt = {0: load_xt(0)}
            sp.dma(d_c, tsb[:, :], tstep.rearrange("(a b) -> a b", a=1).broadcast_to([128, B]))
            t_e = sp.dma(d_c, frq[:, :], freqs)
            sp.wait(t_itk)
            read_experts(0, 1)
            t_wi, t_bi, t_wo, t_x, t_sm = {0: [load_wi_part(i) for i in range(4)]}, {0: load_bi(0)}, {0: load_wo(0)}, {0: load_x(0)}, {0: load_small(0)}
            wstage = {"q": y1, "k": r1, "v": xb[1]}
            wad, bad, emo = qf[0], qr[0][0:B, 0, :], qr[0][0:B, 1, :]
            d_w = slot("w")
            sp.wait(t_e)
            sp.dma(d_w, wad[:, :, :], Wada.rearrange("(k p) n -> p k n", p=128))
            sp.dma(d_w, bad, bada.rearrange("(a n) -> a n", a=1).broadcast_to([B, 2 * D]))
            for n, a in ((0, bq), (1, bk)):
                sp.dma(d_w, bqk[:, n, :], a)
            sp.dma(d_w, bvb[:, :], bv.rearrange("(a n) -> a n", a=1).broadcast_to([128, D]))
            for n, w in (("q", Wq), ("k", Wk), ("v", Wv)):
                t_c = sp.dma(d_w, wstage[n][:, 0:NK, :], w.rearrange("(k p) n -> p k n", p=128))
            read_experts(1, B)
            t_x[1], t_sm[1], t_bi[1] = load_x(1), load_small(1), load_bi(1)

            tk, t_w = {}, {}

            def embed():
                e_, n_, r_, w_ = (em[:, i, 0:B] for i in range(4))
                sc_ = [em[:, 4, 0:B], em[:, 4, B:2 * B]]
                k = dve.op(lambda e: e.tensor_copy(w_, tsb[:, :]), t_e)
                k = dve.op(lambda e: e.tensor_scalar(e_, w_, 0.01, None, ALU.mult), k)
                k = dve.op(lambda e: e.tensor_scalar(n_, e_, 4097.0, None, ALU.mult), k)
                k = dve.op(lambda e: e.tensor_tensor(r_, n_, e_, ALU.subtract), k)
                yield
                k = dve.op(lambda e: e.tensor_tensor(n_, n_, r_, ALU.subtract), k)
                k = dve.op(lambda e: e.tensor_tensor(r_, e_, n_, ALU.subtract), k)
                k = dve.op(lambda e: e.scalar_tensor_tensor(out=w_, in0=n_, scalar=-100.0, in1=w_, op0=ALU.mult, op1=ALU.add), k)
                yield
                k = dve.op(lambda e: e.scalar_tensor_tensor(out=w_, in0=r_, scalar=-100.0, in1=w_, op0=ALU.mult, op1=ALU.add), k)
                k = dve.op(lambda e: e.scalar_tensor_tensor(out=e_, in0=w_, scalar=0.01, in1=e_, op0=ALU.mult, op1=ALU.add), k)
                k = dve.op(lambda e: e.tensor_scalar(e_, e_, 4000.0, None, ALU.mult), k)
                k = dve.op(lambda e: e.tensor_scalar(e_, e_, frq[:, 0:1], None, ALU.mult), k)
                yield
                t_sin = []
                PI = 3.1415925
                for c in range(2):
                    k = dve.op(lambda e, c=c: e.tensor_scalar(n_, e_, 0.15915494309189535, 0.25 * c, ALU.mult, ALU.add), k)
                    k = dve.op(lambda e: e.tensor_scalar(n_, n_, 12582912.0, None, ALU.add), k)
                    k = dve.op(lambda e: e.tensor_scalar(n_, n_, -12582912.0, None, ALU.add), k)
                    yield
                    k = dve.op(lambda e: e.scalar_tensor_tensor(out=r_, in0=n_, scalar=-6.28125, in1=e_, op0=ALU.mult, op1=ALU.add), k)
                    k = dve.op(lambda e: e.scalar_tensor_tensor(out=r_, in0=n_, scalar=-0.0019350051879882812, in1=r_, op0=ALU.mult, op1=ALU.add), k)
                    k = dve.op(lambda e: e.scalar_tensor_tensor(out=r_, in0=n_, scalar=-3.0199159819e-07, in1=r_, op0=ALU.mult, op1=ALU.add), k)
                    yield
                    if c:
                        k = dve.op(lambda e: e.tensor_scalar(r_, r_, 1.5707963267948966, None, ALU.add), k)
                    k = dve.op(lambda e, c=c: e.tensor_scalar(sc_[c], r_, PI, -PI, ALU.min, ALU.max), k)
                    t_sin.append(k)
                t_bad = dve.op(lambda e: e.tensor_scalar(bad[:, 0:D], bad[:, 0:D], 1.0, None, ALU.add), t_c)
                yield
                sn, ex = em[:, 5, :], em[:, 6, :]
                ta = act.op(lambda e: e.activation(sn, em[:, 4, :], ACT.Sin), *t_sin)
                ta = act.op(lambda e: e.activation(ex, sn, ACT.Exp, scale=-1.0), ta)
                act.op(lambda e: e.activation(em[:, 7, :], sn, ACT.Gelu), ta)
                k = dve.op(lambda e: e.tensor_scalar(ex, ex, 1.0, None, ALU.add), ta)
                k = dve.op(lambda e: e.reciprocal(ex, ex), k)
                k = dve.op(lambda e: e.tensor_tensor(ex, ex, sn, ALU.mult), k)
                yield
                for c in range(2):
                    t = pe.op(lambda e, c=c: e.matmul(psQ[0][0:B, :], em[:, 6, c * B:(c + 1) * B], wad[:, c, :], start=c == 0, stop=c == 1),
                              k, t_c, inc=c == 1)
                k = dve.op(lambda e: e.tensor_tensor(emo, psQ[0][0:B, :], bad, ALU.add), t, t_bad)
                k = sp.dma(d_c, sc_ss[:, :], emo, k)
                tk["emb"] = sp.dma(d_c, ss[:, :, :], sc_ss.unsqueeze(0).broadcast_to([128, B, 2 * D]), k)

            def split_small():
                t_w["bq"] = dve.op(lambda e: e.tensor_scalar(bqk[:, 0, :], bqk[:, 0, :], 0.25, None, ALU.mult), t_c)
                for n in "qkv":
                    src, hl = wstage[n][:, 0:NK, :], wsm[n]
                    k = act.op(lambda e, hl=hl, src=src: e.activation(hl[0][:, :, :], src, ACT.Copy), t_c)
                    t_w[n] = dve.op(lambda e, hl=hl, src=src: e.tensor_tensor(hl[1][:, :, :], src, hl[0][:, :, :].bitcast(F32), ALU.subtract), k)

            def split(n, b, src, dst, t_src, q, *free, parts=1, high=act):
                w = src.shape[2] // parts
                t_src = t_src if type(t_src) is list else [t_src] * parts
                for i in range(parts):
                    sl = slice(i * w, (i + 1) * w)
                    if high is act:
                        k = act.op(lambda e, sl=sl: e.activation(dst[0][:, :, sl], src[:, :, sl], ACT.Copy), t_src[i], *free)
                    else:
                        k = dve.op(lambda e, sl=sl: e.tensor_copy(dst[0][:, :, sl], src[:, :, sl]), t_src[i], *free)
                    lo = dve if parts > 1 and i % 2 == 0 else q
                    k = lo.op(lambda e, sl=sl: e.tensor_tensor(dst[1][:, :, sl], src[:, :, sl], dst[0][:, :, sl].bitcast(F32), ALU.subtract), k, *free)
                    tk.setdefault((n, b), []).append(k)

            def split_wi(b, *free, parts=1):
                split("wi", b, wi_f, wi_s, t_wi[b], pool, *free, parts=parts)
                if b + 1 < B:
                    t_wi[b + 1] = load_wi(b + 1, *tk["wi", b])

            def split_wo(b, *free, parts=1):
                split("wo", b, wo_f, wo_s, t_wo[b], pool, *free, parts=parts, high=act if b == 0 else dve)
                if b + 1 < B:
                    t_wo[b + 1] = load_wo(b + 1, *tk["wo", b])

            def split_xt(b, q, *free):
                split("xT", b, xt, xT, t_xt[b], q, *free)
                if b + 1 < B:
                    t_xt[b + 1] = load_xt(b + 1, *tk["xT", b])

            def turn(src, dst, t_src, dst_free):
                for kk in range(NK):
                    for t in range(NT):
                        p = pe.op(lambda e, kk=kk, t=t: e.transpose(psX[:, kk, t * 128:(t + 1) * 128], src[:, t, kk * 128:(kk + 1) * 128], idf[:, :]),
                                  t_src, tk.get("psX"), t_idf, inc=(kk == NK - 1 and t == NT - 1))
                k = act.op(lambda e: e.activation(dst[0][:, :, :], psX[:, :, :], ACT.Copy), p, dst_free)
                tk["psX"] = dve.op(lambda e: e.tensor_tensor(dst[1][:, :, :], psX[:, :, :], dst[0][:, :, :].bitcast(F32), ALU.subtract), k)
                return tk["psX"]

            def turn_q(src, dst, t_src, dst_free):
                for kk in range(NK):
                    for t in range(NT):
                        p = pe.op(lambda e, kk=kk, t=t: e.transpose(psQ[kk][:, t * 128:(t + 1) * 128], src[:, t, kk * 128:(kk + 1) * 128], idf[:, :]),
                                  t_src, tk["psQ", kk], inc=t == NT - 1)
                    k = act.op(lambda e, kk=kk: e.activation(dst[0][:, kk, :], psQ[kk][:, :], ACT.Copy), p, dst_free)
                    tk["psQ", kk] = dve.op(lambda e, kk=kk: e.tensor_tensor(dst[1][:, kk, :], psQ[kk][:, :], dst[0][:, kk, :].bitcast(F32), ALU.subtract), k)
                return tk["psQ", NK - 1]

            def hidden(b, m):
                ms = slice(m * 128, (m + 1) * 128)
                p = mm3(psH[m % 2][:, :], [([w[:, kk, ms] for w in wi_s], [z[:, kk, :] for z in xT]) for kk in range(NK)],
                        tk["wi", b][m * len(tk["wi", b]) // NM], *tk["xT", b], tk.get(("gelu_ps", m % 2)))
                f = hf[m % 3]
                g = act.op(lambda e: e.activation(f[:, :], psH[m % 2][:, :], ACT.Gelu, bias=bis[b % 2][:, m:m + 1]),
                           p, t_bi[b], tk.get(("hf", m % 3)))
                tk["gelu_ps", m % 2] = g
                k = act.op(lambda e: e.activation(hT[0][:, m, :], f[:, :], ACT.Copy), g, tk.get(("O", b - 1)))
                k = dve.op(lambda e: e.tensor_tensor(hT[1][:, m, :], f[:, :], hT[0][:, m, :].bitcast(F32), ALU.subtract), k)
                tk["hf", m % 3] = k
                tk["H", b] = p
                tk.setdefault(("hT", b), []).append(k)
                if m == NM - 1 and b + 2 < B:
                    t_bi[b + 2] = load_bi(b + 2, g)

            def down(b, t):
                ts = slice(t * 128, (t + 1) * 128)
                tk["O", b] = mm3(psO[:, t, :], [([z[:, m, ts] for z in hT], [w[:, m, :] for w in wo_s]) for m in range(NM)],
                                 *tk["wo", b], tk.get(("r1", b - 1)), each=tk["hT", b])

            def add_bo(b):
                tk["xb", b] = pool.op(lambda e: e.tensor_tensor(xb[b % 2][:, :, :], xs[b % 2][:, :, :], bc(ob[b % 2][:, 0, :], NT), ALU.add),
                                      t_x[b], t_sm[b], tk.get(("r1", b - 2)), t_w["v"] if b else None)
                if b + 2 < B:
                    t_x[b + 2] = load_x(b + 2, tk["xb", b])

            def norms(b):
                o = ob[b % 2]
                k = dve.op(lambda e: e.tensor_tensor(r1[:, :, :], psO[:, :, :], xb[b % 2][:, :, :], ALU.add), tk["xb", b], tk["O", b], t_w["k"])
                tk["r1", b] = k
                yield
                k = yield from layernorm(r1, y1, stt, mv, sm, 1e-12, o[:, 1, :], o[:, 2, :], k, t_w["q"], t_sm[b])
                if b + 2 < B:
                    t_sm[b + 2] = load_small(b + 2, k, tk["xb", b])
                z = x2[b % 2]
                tk["x2", b] = yield from layernorm(y1, z, stt, mv, sm, 1e-5, ss[:, b, 0:D], ss[:, b, D:2 * D], k,
                                                   tk.get(("x2T", b - 2)), tk.get(("sx2", b - 2)), tk["emb"])
                tk["sx2", b] = sp.dma(d_x2[b % 2], rows(sc_x2[b]), z[:, :, :], tk["x2", b])

            d_p, d_v, d_x2 = [slot(f"p{i}") for i in range(2)], slot("v"), [slot(f"x2{i}") for i in range(2)]

            def qkv(b):
                def low(n, k):
                    pt = parts[n]
                    k = act.op(lambda e: e.activation(pt[:, 1, :, :], qr[n][:, :, :], ACT.Copy), k)
                    k = pool.op(lambda e: e.tensor_tensor(pt[:, 2, :, :], qr[n][:, :, :], pt[:, 1, :, :], ALU.subtract), k)
                    tk["qr", n] = k
                    def store():
                        for c in range(3):
                            tk["parts", n] = sp.dma(d_p[n], sc_qk[b, n, c].rearrange("(k p) s -> p k s", p=128), pt[:, c, :, :], k)
                    if b < B - 1:
                        store()
                    else:
                        left["stores"].append(store)

                rest = []
                for n, (w, scale) in enumerate((("q", 0.25), ("k", 1.0))):
                    for mt in range(NK):
                        ms = slice(mt * 128, (mt + 1) * 128)
                        p = mm3(psQ[mt][:, :], [([u[:, kk, ms] for u in wsm[w]], [z[:, kk, :] for z in x2T]) for kk in range(NK)],
                                t_w[w], tk["x2T", b], tk.get(("psQ", mt)), tk["emb"])
                        k = act.op(lambda e, mt=mt, n=n, scale=scale: e.activation(qf[n][:, mt, :], psQ[mt][:, :], ACT.Identity,
                                                                                   bias=bqk[:, n, mt:mt + 1], scale=scale),
                                   p, t_w["bq"], tk.get(("qf", n)), tk["emb"])
                        tk["psQ", mt] = k
                        yield
                    pt = parts[n]
                    k = act.op(lambda e, pt=pt, n=n: e.activation(pt[:, 0, :, :], qf[n][:, :, :], ACT.Copy), k, tk.get(("parts", n)))
                    k = dve.op(lambda e, pt=pt, n=n: e.tensor_tensor(qr[n][:, :, :], qf[n][:, :, :], pt[:, 0, :, :], ALU.subtract),
                               k, tk.get(("qr", n)), tk["emb"])
                    tk["qf", n] = k
                    rest.append(k)
                    if n:
                        low(0, rest[0])
                for half in range(2):
                    for t in (2 * half, 2 * half + 1):
                        ts = slice(t * 128, (t + 1) * 128)
                        p = mm3(psQ[half][:, (t % 2) * D:(t % 2 + 1) * D],
                                [([z[:, kk, ts] for z in x2T], [u[:, kk, :] for u in wsm["v"]]) for kk in range(NK)],
                                t_w["v"], tk.get(("psQ", half)))
                    for t in (2 * half, 2 * half + 1):
                        k = dve.op(lambda e, t=t, half=half: e.tensor_tensor(
                            v17[:, t, :, 0:HD], psQ[half][:, (t % 2) * D:(t % 2 + 1) * D].rearrange("p (h d) -> p h d", d=HD),
                            bvb[:, :].rearrange("p (h d) -> p h d", d=HD), ALU.add), p, tk.get("sv"), t_c)
                    tk["psQ", half] = k
                    if half == 0:
                        low(1, rest[1])
                    yield
                tk["V", b] = p
                tk["sv"] = sp.dma(d_v, rows(sc_v[b]), v17[:, :, :, :].rearrange("p t h v -> p t (h v)"), k, t_one)
                left["batch", b] = [tk["parts", 0], tk["parts", 1], tk["sv"]]

            split_xt(0, dve)
            split_wi(0, parts=4)
            t_one = dve.op(lambda e: e.memset(v17[:, :, :, HD:VW], 1.0))
            side = embed()
            for i in range(B):
                if i >= 1:
                    side = norms(i - 1)
                    advance(side, 1)
                for m in range(NM):
                    hidden(i, m)
                    if m == 3 and i >= 2:
                        tk["x2T", i - 2] = turn(x2[i % 2], x2T, tk["x2", i - 2], tk.get(("V", i - 3)))
                    advance(side, 1 if i == 0 else ASIDE[0] if m > 3 else 0)
                    if m == 0:
                        split_wo(i, tk.get(("O", i - 1)), parts=1 if i else 4)
                        add_bo(i)
                q = qkv(i - 2) if i >= 2 else iter(())
                for n in range(6):
                    advance(q, 1)
                    advance(side, 3 if i else 0)
                    if n == 3 and i + 1 < B:
                        split_xt(i + 1, pool, tk["H", i])
                        split_wi(i + 1, tk["H", i])
                advance(q, 1)
                for t in range(NT):
                    down(i, t)
                    advance(side, ASIDE[2] if i else t % 2)
                    if i == 0 and t == 1:
                        split_small()
                advance(side, 1000)
            left["O"] = tk["O", B - 1]
            yield
            side = norms(B - 1)
            advance(side, 6)
            tk["x2T", B - 2] = turn(x2[B % 2], x2T, tk["x2", B - 2], tk["V", B - 3])
            left["first"] = [tk["psX"], tk["r1", B - 1]]
            yield
            q = qkv(B - 2)
            for n in range(7):
                advance(q, 1)
                advance(side, 3)
                yield
            advance(side, 1000)
            tk["x2T", B - 1] = turn_q(x2[(B - 1) % 2], x2T, tk["x2", B - 1], tk["V", B - 2])
            yield
            q = qkv(B - 1)
            for n in range(7):
                advance(q, 1)
                yield
            left["psum"] = [tk["psQ", 0], tk["psQ", 1]]

        def phase_b(st):
            def sb(name, shape, dt=F32):
                return sbuf(st, name, shape, dt)

            NB, NP, NS, NTB, EARLY, MORE = 5, 6, 4, 3, 5, 21
            psS = [st.enter_context(nc.psum_tensor(f"psS{i}", [128, 512], F32)) for i in range(3)]
            psT = [st.enter_context(nc.psum_tensor(f"psT{i}", [128, NT, 128], F32)) for i in range(NTB)]
            psV = st.enter_context(nc.psum_tensor("psV", [128, 512], F32))
            psS.append(st.enter_context(nc.psum_tensor("psS3", [128, 512], F32)))
            psC = psV.rearrange("p (t g d) -> p t g d", t=NT, g=4)

            bt = [sb(f"bt{i}", [128, NT, S]) for i in range(NB)]
            qs, ks = [sb("qs0", [KR, 8, S], BF16)], [sb("ks0", [KR, 8, S], BF16)]
            mk, mb = [sb("mk0", [128, NT, S], U8)], [sb("mb0", [128, NT, S], BF16)]
            vs = [sb("vs0", [128, NT, H, VW])]
            nm = sb("nm", [128, 16])
            pt = [sb(f"pt{i}", [128, NT, S]) for i in range(EARLY)]
            pt += [sb(f"pt{i}", [128, NT, S]) for i in range(EARLY, NP)]
            qs.append(sb("qs1", [KR, 8, S], BF16))
            ks.append(sb("ks1", [KR, 8, S], BF16))
            mk.append(sb("mk1", [128, NT, S], U8))
            mb.append(sb("mb1", [128, NT, S], BF16))
            vs.append(sb("vs1", [128, NT, H, VW]))
            na = [sb(f"na{i}", [128, NT]) for i in range(2)]
            den = sb("den", [128, NT, H])
            cv = sb("cv", [128, 512])
            cr = sb("cr", [128, NT, H, VW])
            cx = [sb(f"cx{i}", [128, NT, D]) for i in range(2)]
            wl.update({n: [sb(f"cw{n}{p}", [128, k, w], F32R) for p in "hl"] for n, (_, k, w) in ws.items()})
            wl["rb"], wl["b1"] = sb("rb", [128, 4, D]), sb("b1c", [128, NM])
            wf = sb("wf", [128, NK * I])
            d_b = [slot(f"b{i}") for i in range(NB)]
            d_q = [slot(f"q{i}") for i in range(2)]
            d_m, d_v = ([slot(f"{n}{i}") for i in range(2)] for n in ("m", "vb"))
            d_o = [slot(f"o{i}") for i in range(2)]
            N = B * H * NT
            tk = {}
            def load_qk(n):
                b, half = divmod(n, 2)
                free = tk.get(("QK", 32 * (n - 1) - 1))
                for dst, w in ((qs, 0), (ks, 1)):
                    for i, c in enumerate(TERMS):
                        src = sc_qk[b, w, c[w]].rearrange("(h d) s -> d h s", d=HD)[:, 8 * half:8 * half + 8, :]
                        tk["qs", n] = sp.dma(d_q[n % 2], dst[n % 2][i * HD:(i + 1) * HD, :, :], src, free,
                                             *(left["batch", 0] + [left["O"]] if n == 0 else left["psum"] if n == 1 else left["batch", 1] if n < 4 else ()))

            def load_mask(b):
                free = [tk.get(("mb", b - 2)), tk.get(("na", b - 2))] if b > 1 else left["psum"] if b else [left["O"]]
                tk["vm", b] = sp.dma(d_m[b % 2], mk[b % 2][:, :, :], rows(mask[b]), *free)

            def load_v(b):
                early = left["batch", b] + (left["psum"] if b else [])
                tk["vs", b] = sp.dma(d_v[b % 2], vs[b % 2][:, :, :, :].rearrange("p t h v -> p t (h v)"), rows(sc_v[b]),
                                      *([tk.get(("PV", 4 * (b - 1) - 1))] if b else [left["O"]]), *(early if b < 2 else []))

            def read_mask(b, t):
                free = [tk.get(("QK", 64 * (b - 1) - 1)), tk.get(("M", 16 * (b - 1) - 1)), tk.get(("M", 16 * (b - 1) - 2))]
                m, dst, top = mk[b % 2][:, t, :], mb[b % 2][:, t, :], na[b % 2][:, t:t + 1]
                if b:
                    tk["mb", b] = dve.op(lambda e: e.tensor_tensor_reduce(dst, m, m, NEG, -3.0e38, ALU.mult, ALU.max, top),
                                         tk["vm", b], tk.get(("nd", b - 2)), *free)
                else:
                    tk["mb", b] = act.op(lambda e: e.activation(dst, m, ACT.Copy, scale=NEG), tk["vm", b], *free)

            def read_any(b):
                if b == 0:
                    k = dve.op(lambda e: e.tensor_reduce(na[0][:, :], mb[0][:, :, :], AX.X, ALU.max), tk["mb", b])
                else:
                    k = tk["mb", b]
                tk["na", b] = dve.op(lambda e: e.tensor_scalar(na[b % 2][:, :], na[b % 2][:, :], 0.0, None, ALU.is_ge), k)

            def load_bias(u):
                tk["bt", u] = sp.dma(d_b[u % NB], bt[u % NB][:, :, :], rows(bias[u // H, u % H]),
                                     tk.get(("T", 4 * (u - NB) + 3)) if u >= NB else left["O"])

            def on_pool(u):
                return u % 4 != 3

            def add_mask(u):
                t, m = bt[u % NB], mb[u // H % 2]
                for i in range(2):
                    hs = slice(2 * i, 2 * i + 2)
                    tk["M", u, i] = pool.op(lambda e, hs=hs: e.tensor_tensor(t[:, hs, :], t[:, hs, :], m[:, hs, :], ALU.add), tk["bt", u], tk["mb", u // H])
                tk["M", u] = tk["M", u, 1]

            def bank(n):
                return n % 3 if n < MORE else (n - MORE - 1) % NS

            def scores(n):
                u, t = divmod(n, NT)
                b, h = divmod(u, H)
                g = u // 8 % 2
                ts = slice(t * 128, (t + 1) * 128)
                if not on_pool(u):
                    pe.op(lambda e: e.matmul(psS[bank(n)][:, :], idb[:, :], mb[b % 2][:, t, :], start=True, stop=False),
                          tk["mb", b], tk.get(("exp", n - (3 if n < MORE else NS))), t_idb, inc=False)
                tk["QK", n] = pe.op(lambda e: e.matmul(psS[bank(n)][:, :], qs[g][:, h % 8, ts], ks[g][:, h % 8, :], start=on_pool(u), stop=True),
                                    tk["qs", u // 8], tk.get(("exp", n - (3 if n < MORE else NS))))
                s = bt[u % NB][:, t, :]
                tk["max", n] = dve.op(lambda e: e.tensor_tensor_reduce(psS[bank(n)][:, :], psS[bank(n)][:, :], s, -1.0, 3.0e38, ALU.add, ALU.min,
                                                                       nm[:, n % 16:n % 16 + 1]),
                                      tk["QK", n], tk["bt", u], tk.get(("M", u, t // 2)), tk.get(("exp", n - 16)))

            def exps(n):
                s = bt[n // NT % NB][:, n % NT, :]
                tk["exp", n] = act.op(lambda e: e.activation(s, psS[bank(n)][:, :], ACT.Exp, bias=nm[:, n % 16:n % 16 + 1], scale=-1.0), tk["max", n])

            def turn_p(n):
                u, t = divmod(n, NT)
                for kk in range(NT):
                    tk["T", n] = pe.op(lambda e, kk=kk: e.transpose(psT[n % NTB][:, kk, :], bt[u % NB][:, t, kk * 128:(kk + 1) * 128], idf[:, :]),
                                       tk["exp", n], tk.get(("E", n - NTB)), inc=kk == NT - 1)

            def evac(n):
                u, t = divmod(n, NT)
                dst, src = pt[u % NP][:, :, t * 128:(t + 1) * 128], psT[n % NTB][:, :, :]
                if n % 5 in ON_ACT:
                    q, f = act, lambda e: e.activation(dst, src, ACT.Copy)
                else:
                    q, f = dve, lambda e: e.tensor_copy(dst, src)
                tk["E", n] = q.op(f, tk["T", n], *([tk["PV", (u - NP) // 4]] if u >= NP else left["psum"] if u >= EARLY else []))
                tk["Es", u] = tk.get(("Es", u), []) + [tk["E", n]]

            def context(gi, kk):
                b, hg = divmod(gi, 4)
                for g in range(4):
                    u = 4 * gi + g
                    p = pe.op(lambda e, g=g, u=u: e.matmul(
                        psV[32 * g:32 * g + VW, :], vs[b % 2][:, kk, u % H, :], pt[u % NP][:, kk, :], start=kk == 0, stop=kk == NT - 1),
                        *tk["Es", u], tk["vs", b], tk.get(("C", gi - 1)), t_vz, inc=(kk == NT - 1 and g == 3))
                if kk == NT - 1:
                    tk["PV", gi] = p
                    tk["cv", gi] = act.op(lambda e: e.activation(cv[:, :], psV[:, :], ACT.Copy), p, tk.get(("CT", gi - 1)))

            def finish(gi):
                b, hg = divmod(gi, 4)
                for t in range(NT):
                    p = pe.op(lambda e, t=t: e.transpose(psC[:, t, :, :].rearrange("p a c -> p (a c)"), cv[:, t * 128:(t + 1) * 128], idf[:, :]),
                              tk["cv", gi], tk.get(("C", gi - 1)), inc=t == NT - 1)
                tk["CT", gi] = p
                tk["C", gi] = dve.op(lambda e: e.tensor_copy(cr[:, :, 4 * hg:4 * hg + 4, :], psC[:, :, :, 0:VW]), p, tk.get(("n", b - 1)))
                if hg == 3:
                    nb = na[b % 2][:, :].unsqueeze(2).broadcast_to([128, NT, H])
                    k = dve.op(lambda e: e.tensor_tensor(den[:, :, :], cr[:, :, :, HD], nb, ALU.mult), tk["C", gi], tk["na", b], tk.get(("n", b - 1)))
                    k = dve.op(lambda e: e.reciprocal(den[:, :, :], den[:, :, :]), k)
                    k = dve.op(lambda e: e.tensor_tensor(den[:, :, :], den[:, :, :], nb, ALU.mult), k)
                    tk["nd", b] = k
                    tk["n", b] = pool.op(lambda e: e.tensor_tensor(cx[b % 2][:, :, :].rearrange("p t (h d) -> p t h d", d=HD), cr[:, :, :, 0:HD],
                                                                   den[:, :, :].unsqueeze(3).broadcast_to([128, NT, H, HD]), ALU.mult),
                                         k, tk.get(("so", b - 2)))

            def store(b):
                left["so", b] = tk["so", b] = sp.dma(d_o[b % 2], rows(sc_c[b]), cx[b % 2][:, :, :], tk["n", b])

            d_w = slot("cw")

            def load_w(n):
                w, k, wd = ws[n]
                tk["wf", n] = sp.dma(d_w, wf[:, 0:k * wd].rearrange("p (k n) -> p k n", n=wd), w.rearrange("(k p) n -> p k n", p=128), tk.get("wl"))

            def split_w(n, c):
                cs = slice(c * 512, (c + 1) * 512)
                hi, lo = (a.rearrange("p k n -> p (k n)")[:, cs] for a in wl[n])
                k = act.op(lambda e: e.activation(hi, wf[:, cs], ACT.Copy), tk["wf", n])
                left["w", n] = tk["wl"] = pool.op(lambda e: e.tensor_tensor(lo, wf[:, cs], hi.bitcast(F32), ALU.subtract), k)

            extra, at = {}, 100
            for n, (w, k, wd) in ws.items():
                extra[at] = lambda n=n: load_w(n)
                for c in range(k * wd // 512):
                    at += 10
                    extra[at] = lambda n=n, c=c: split_w(n, c)
                at += 16

            load_mask(0)
            load_bias(0)
            load_qk(0)
            for u in range(1, NB):
                load_bias(u)
            load_v(0)
            yield
            for t in range(NT):
                read_mask(0, t)
            LAG, ELAG, XLAG, PSTEP, ON_ACT = 4, 0, 1, 2, (0, 2, 4)
            nextb, nextm, FIRST = NB, 0, 20
            SLAG = 12
            yield
            pe.wait(*left["first"])
            for n in range(N + 40):
                while nextb < min(B * H, n // NT + NB) and (nextb < NB or ("T", 4 * (nextb - NB) + 3) in tk):
                    load_bias(nextb)
                    nextb += 1
                while nextm < min(B * H, n // NT + 3, nextb) and ("mb", nextm // H) in tk:
                    if on_pool(nextm):
                        add_mask(nextm)
                    nextm += 1
                if n == 19:
                    ends = [(q.sem, q.n) for q in (pe, act, dve, pool)]
                    dve.wait(*left["psum"])
                    pe.wait(*left["psum"])
                    t_vz = dve.op(lambda e: e.memset(psV[:, :], 0.0))
                if n == 44:
                    for late in left["stores"]:
                        late()
                    turn_over()
                if n == 48:
                    sp.wait(*ends, *[(s[0], s[1]) for s in a_slots])
                if n in extra:
                    extra[n]()
                if n == 68:
                    for i, a in enumerate((bo, g2, be2, b2)):
                        sp.dma(d_w, wl["rb"][:, i, :], a.rearrange("(a n) -> a n", a=1).broadcast_to([128, D]))
                    left["rb"] = sp.dma(d_w, wl["b1"][:, :], b1)
                if n == 39:
                    read_any(0)
                if n < N and n % 32 == (4 if n > 32 else FIRST) and n // 32 + 1 < 2 * B:
                    load_qk(n // 32 + 1)
                if n < N and n % 64 == 28 and n // 64 + 1 < B:
                    load_mask(n // 64 + 1)
                    load_v(n // 64 + 1)
                if n < N and n // 64 + 1 < B and n % 4 == 1 and 33 <= n % 64 < 49:
                    read_mask(n // 64 + 1, n % 64 // 4 - 8)
                if 64 < n < N and n % 64 == 7:
                    read_any(n // 64)
                if n == 3 * N // 4:
                    left["load_c"]()
                if n < N:
                    scores(n)
                m = n - LAG
                if 0 <= m < N:
                    turn_p(m)
                m = n - LAG - ELAG
                if 0 <= m < N:
                    evac(m)
                m = n - XLAG
                if 0 <= m < N:
                    exps(m)
                for kk in range(NT):
                    m = n - LAG - ELAG - 1 - PSTEP * kk
                    if 0 <= m < N and m % 16 == 15:
                        context(m // 16, kk)
                m = n - LAG - ELAG - 3 - 3 * PSTEP
                if 0 <= m < N and m % 16 == 15:
                    finish(m // 16)
                m -= SLAG
                if 0 <= m < N and m % 64 == 63:
                    store(m // 64)
                if n < 19:
                    yield
                if n == N - 1 + LAG + ELAG:
                    left["S"] = [tk["exp", N - 1 - i] for i in range(NS)]
                    left["T"] = [tk["E", N - 1 - i] for i in range(NTB)]
                    left["P"] = tk["T", N - 1]
                    yield
                if n == N + LAG + ELAG + 3 * PSTEP:
                    yield
            left["V"] = [tk["cv", N // 16 - 1], tk["C", N // 16 - 1]]

        def phase_c(st):
            def sb(name, shape, dt=F32):
                return sbuf(st, name, shape, dt)

            psX = st.enter_context(nc.psum_tensor("psX2", [128, NK, 512], F32))
            psA = st.enter_context(nc.psum_tensor("psA2", [128, NT, D], F32))
            psH = [st.enter_context(nc.psum_tensor(f"psH2{i}", [128, 512], F32)) for i in range(2)]
            psO = st.enter_context(nc.psum_tensor("psO2", [128, NT, D], F32))
            cs, xs = [sb("cin1", [128, NT, D])], [sb("rin1", [128, NT, D])]
            cT = [sb(f"cT{n}", [128, NK, S], F32R) for n in "hl"]
            lT = [sb(f"lT{n}", [128, NK, S], F32R) for n in "hl"]
            hf = [sb(f"chf{i}", [128, S]) for i in range(3)]
            hT = [sb(f"chT{n}", [128, NM, S], F32R) for n in "hl"]
            x3 = [sb(f"x3{i}", [128, NT, D]) for i in range(2)]
            hl = [sb(f"hl{i}", [128, NT, D]) for i in range(2)]
            warm = sb("warm", [128, NM])
            stt, mv, sm = sb("cstt", [128, NT, 6]), sb("cmv", [128, NT, 2]), sb("csm", [128, 4, NT])
            os_ = [sb(f"os{i}", [128, NT, D]) for i in range(2)]
            sb("clear", [128, CLEAR])
            cs.insert(0, sb("cin0", [128, NT, D]))
            xs.insert(0, sb("rin0", [128, NT, D]))
            d_l, d_r, d_out = ([slot(f"{n}{i}") for i in range(2)] for n in ("cl", "cr", "out"))
            tk = {}

            def load_ctx(b, *waits):
                tk["cs", b] = sp.dma(d_l[b % 2], cs[b % 2][:, :, :], rows(sc_c[b]), left["so", b], *waits)

            def load_x2(b, *waits):
                tk["xs", b] = sp.dma(d_r[b % 2], xs[b % 2][:, :, :], rows(sc_x2[b]), *waits)

            def turn(src, dst, t_src, *dst_free):
                for kk in range(NK):
                    for t in range(NT):
                        p = pe.op(lambda e, kk=kk, t=t: e.transpose(psX[:, kk, t * 128:(t + 1) * 128], src[:, t, kk * 128:(kk + 1) * 128], idf[:, :]),
                                  t_src, tk.get("psX"), inc=(kk == NK - 1 and t == NT - 1))
                k = act.op(lambda e: e.activation(dst[0][:, :, :], psX[:, :, :], ACT.Copy), p, *dst_free)
                k = dve.op(lambda e: e.tensor_tensor(dst[1][:, :, :], psX[:, :, :], dst[0][:, :, :].bitcast(F32), ALU.subtract), k)
                tk["psX"] = k
                return k

            def residual(b):
                tk["x3", b] = dve.op(lambda e: e.tensor_tensor(x3[b % 2][:, :, :], psA[:, :, :], xs[b % 2][:, :, :], ALU.add),
                                     tk["xb", b], tk["A", b], tk.get(("out", b - 2)))
                if b + 2 < B:
                    load_x2(b + 2, tk["x3", b])

            def norms(b):
                h = hl[b % 2]
                k = yield from layernorm(x3[b % 2], h, stt, mv, sm, 1e-5, rb[:, 1, :], rb[:, 2, :], tk["x3", b], tk.get(("lT", b - 2)))
                tk["h", b] = k
                tk["x3b", b] = pool.op(lambda e: e.tensor_tensor(x3[b % 2][:, :, :], x3[b % 2][:, :, :], bc(rb[:, 3, :], NT), ALU.add), k)

            def turn_c(b):
                dst = lT if b == 1 else cT
                tk["cT", b] = turn(cs[b % 2], dst, tk["cs", b], tk.get(("A", b - 1)) if b != 1 else None)
                if b + 2 < B:
                    load_ctx(b + 2, tk["cT", b])

            def add_bo(b):
                tk["xb", b] = pool.op(lambda e: e.tensor_tensor(xs[b % 2][:, :, :], xs[b % 2][:, :, :], bc(rb[:, 0, :], NT), ALU.add),
                                      tk["xs", b], left["rb"])

            def project(b, t):
                ts = slice(t * 128, (t + 1) * 128)
                tk["A", b] = mm3(psA[:, t, :], [([z[:, kk, ts] for z in (lT if b == 1 else cT)], [u[:, kk, :] for u in wl["o"]]) for kk in range(NK)],
                                 tk["cT", b], left["w", "o"], tk.get(("x3", b - 1)))

            def turn_l(b):
                tk["lT", b] = turn(hl[b % 2], lT, tk["h", b], tk["H", b - 1] if b else tk["A", 1])

            def up(b, m):
                ms = slice(m * 128, (m + 1) * 128)
                p = mm3(psH[m % 2][:, :], [([w[:, kk, ms] for w in wl["1"]], [z[:, kk, :] for z in lT]) for kk in range(NK)],
                        left["w", "1"], tk["lT", b], tk.get(("g", m % 2)))
                f = hf[m % 3]
                g = act.op(lambda e: e.activation(f[:, :], psH[m % 2][:, :], ACT.Gelu_apprx_sigmoid, bias=b1c[:, m:m + 1]),
                           p, left["rb"], tk.get(("hf", m % 3)))
                tk["g", m % 2] = g
                k = act.op(lambda e: e.activation(hT[0][:, m, :], f[:, :], ACT.Copy), g, tk.get(("O", b - 1)))
                k = dve.op(lambda e: e.tensor_tensor(hT[1][:, m, :], f[:, :], hT[0][:, m, :].bitcast(F32), ALU.subtract), k)
                tk["hf", m % 3] = k
                tk["H", b] = p
                tk.setdefault(("hT", b), []).append(k)

            def down(b, t):
                ts = slice(t * 128, (t + 1) * 128)
                tk["O", b] = tk["O", b, t] = mm3(psO[:, t, :], [([z[:, m, ts] for z in hT], [w[:, m, :] for w in wl["2"]]) for m in range(NM)],
                                 left["w", "2"], tk.get(("out", b - 1)), each=tk["hT", b])

            def store_last(b):
                for i in range(2):
                    hs = slice(2 * i, 2 * i + 2)
                    k = dve.op(lambda e, hs=hs: e.tensor_tensor(os_[b % 2][:, hs, :], psO[:, hs, :], x3[b % 2][:, hs, :], ALU.add),
                               tk["O", b, 2 * i + 1], tk["x3b", b], tk.get(("so", b - 2)))
                    sp.dma(d_out[b % 2], rows(out[b])[:, hs, :], os_[b % 2][:, hs, :], k)

            def store(b):
                k = dve.op(lambda e: e.tensor_tensor(os_[b % 2][:, :, :], psO[:, :, :], x3[b % 2][:, :, :], ALU.add),
                           tk["O", b], tk["x3b", b], tk.get(("so", b - 2)))
                tk["out", b] = k
                tk["so", b] = sp.dma(d_out[b % 2], rows(out[b]), os_[b % 2][:, :, :], k)

            rb, b1c = wl["rb"], wl["b1"]

            def load_first():
                load_ctx(0, left["w", "2"])
                load_x2(0, left["w", "2"])
            left["load_c"] = load_first
            yield
            load_ctx(1, left["P"])
            load_x2(1, left["P"])
            pe.wait(*left["S"])
            turn_c(0)
            add_bo(0)
            yield
            pe.wait(*left["T"])
            turn_c(1)
            for t in range(NT):
                project(0, t)
            residual(0)
            advance(norms(0), 1000)
            act.op(lambda e: e.activation(warm[:, :], b1c[:, :], ACT.Gelu_apprx_sigmoid), left["rb"])
            add_bo(1)
            yield
            ends = turn_over()
            sp.wait(*ends)
            for t in range(NT):
                project(1, t)
            turn_l(0)
            pe.wait(*left["V"])
            for b in range(B):
                if b:
                    store(b - 1)
                side = iter(())
                if b < B - 1:
                    residual(b + 1)
                    side = norms(b + 1)
                for m in range(NM):
                    up(b, m)
                    if m == 3 and b + 2 < B:
                        turn_c(b + 2)
                        add_bo(b + 2)
                    advance(side, SIDE[0] if m > 3 else 0)
                for t in range(NT if b + 2 < B else 0):
                    project(b + 2, t)
                    advance(side, SIDE[1])
                for t in range(NT - 1):
                    down(b, t)
                    advance(side, SIDE[2])
                advance(side, 1000)
                if b + 1 < B:
                    turn_l(b + 1)
                down(b, NT - 1)
            store_last(B - 1)
            yield

        MIX = [0, 0, 1, 2, 1, 1, 2, 2, 1, 1, 1, 1, 1, 1, 1]
        CLEAR, ASIDE, SIDE = 28000, (1, 2, 3), (1, 2, 3)
        ws, wl = {"o": (Wo, NK, D), "1": (W1, NK, I), "2": (W2, NM, D)}, {}
        with ExitStack() as st:
            a = phase_a(st)
            next(a)
        a_slots = list(slots)
        with ExitStack() as st:
            b = phase_b(st)
            next(b)
        next(a)
        next(b)
        for steps in MIX:
            advance(a, 1)
            advance(b, steps)
        advance(a, 1)
        advance(b, 19 - sum(MIX))
        with ExitStack() as st:
            c = phase_c(st)
            next(c)
        next(b)
        next(c)
        next(b)
        next(c)
        advance(b, 1)
        advance(c, 3)
        sp.wait(*[(s[0], s[1]) for s in slots if s[1]])

        block = ctx.enter_context(nc.Block())

        @block.sync
        def _(e):
            sp.emit(e)

        @block.tensor
        def _(e):
            pe.emit(e)

        @block.scalar
        def _(e):
            act.emit(e)

        @block.vector
        def _(e):
            dve.emit(e)

        @block.gpsimd
        def _(e):
            pool.emit(e)


_INS = ["x", "itok_B_0_7", "itok_B_34_63", "fside_Bx16xSxS_0", "mask_Bx1xSxS_bk0",
        "L0_cond_Wi", "L0_cond_bi", "L0_cond_Wo", "L0_cond_bo", "L0_cond_gamma", "L0_cond_beta",
        "L1_cond_W_ada", "L1_cond_b_ada", "L1_cond_Wq", "L1_cond_bq", "L1_cond_Wk", "L1_cond_bk",
        "L1_cond_Wv", "L1_cond_bv", "L1_cond_Wo", "L1_cond_bo", "L1_cond_W1", "L1_cond_b1",
        "L1_cond_W2", "L1_cond_b2", "L1_cond_g2", "L1_cond_beta2"]
_COLS = ["L0_cond_bi", "L1_cond_bq", "L1_cond_bk", "L1_cond_b1"]


def kernel(**inputs):
    import numpy as np
    import concourse.bacc as bacc
    from concourse.bass_utils import run_bass_kernel_spmd as run

    nc = bacc.Bacc("TRN2", target_bir_lowering=False, num_devices=1)
    arrays, args = {}, []

    def give(name, a):
        arrays[name] = a
        args.append(nc.dram_tensor(name, a.shape, mybir.dt.from_np(a.dtype), kind="ExternalInput").ap())

    for name in _INS:
        a = np.ascontiguousarray(inputs[name])
        if name.startswith("mask"):
            a = a.reshape(B, S, S)
        if name in _COLS:
            a = np.ascontiguousarray(np.swapaxes(a.reshape(a.shape[:-1] + (-1, 128)), -1, -2))
        give(f"in_{name}", a)
    a = np.ascontiguousarray(np.swapaxes(np.asarray(inputs["x"]), 1, 2))
    arrays["in_x_t"] = a
    args.insert(1, nc.dram_tensor("in_x_t", a.shape, F32, kind="ExternalInput").ap())
    give("ident", np.eye(128, dtype=np.float32))
    step = np.float32(-np.log(10000.0) / 127)
    give("freqs", np.exp(np.arange(128, dtype=np.float32) * step).astype(np.float32).reshape(128, 1))
    args.append(nc.dram_tensor("out_0", (B, S, D), F32, kind="ExternalOutput").ap())
    program(nc, *args)
    r = run(nc, [arrays], core_ids=[0])
    return r.results[0]["out_0"]
```
